# Optimizing a Trainium2 kernel written in Bass

```python
import numpy as np
import jax
import jax.numpy as jnp

def _softmax(x, axis=-1):
    return jax.nn.softmax(x, axis=axis)

def _gelu(x):
    return jax.nn.gelu(x, approximate=True)

def _silu(x):
    return jax.nn.silu(x)

def _sigmoid(x):
    return jax.nn.sigmoid(x)

def _layernorm(x, axis=-1, eps=1e-05):
    m = jnp.mean(x, axis=axis, keepdims=True)
    v = jnp.var(x, axis=axis, keepdims=True)
    return (x - m) / jnp.sqrt(v + eps)

def _scatter_add(tgt, idx, src, axis=0):
    return tgt.at[idx].add(src)

def _segment_sum(src, seg, n):
    return jax.ops.segment_sum(src, seg, n)
kernel_name = 'mk_adj_preln_d1_adj_r2_6f37b6'

def setup_inputs(seed: int=0):
    np.random.seed(seed)
    _w = jnp.asarray

    def _rec_inputs():
        import jax
        import jax.numpy as jnp
        _gk = jax.random.key(seed)
        x = -0.0005207 + 1.001 * jax.random.normal(jax.random.fold_in(_gk, 1), (4096, 128), jnp.float32)
        _a = jax.random.bernoulli(jax.random.fold_in(_gk, 2), 0.000976562, (4096, 4096))
        _a = jnp.logical_or(_a, jnp.swapaxes(_a, -1, -2))
        _a = jnp.logical_or(_a, jnp.eye(4096, dtype=bool))
        _af = _a.astype(jnp.float32)
        _af = _af * jax.random.uniform(jax.random.fold_in(_gk, 3), (4096, 4096), jnp.float32, 0.05, 1)
        adj = _af
        return (x, adj)
    x, adj = _rec_inputs()

    def _L0_gnn_setup():
        import jax, jax.numpy as jnp
        import numpy as np
        D_IN = 128
        D_ATTN = 64
        STEPS = 2
        TOP_P = 0.9
        TAU = 1.0
        LN_EPS = 1e-05
        N_NODES = 4096

        def _top_p_attention(X, W1, W2, W3):
            q = X @ W1.T @ W2.T
            k = X @ W3.T
            logits = q @ k.T / TAU
            probs = jax.nn.softmax(logits, axis=-1)
            idx = jnp.argsort(-probs, axis=-1)
            sp = jnp.take_along_axis(probs, idx, axis=-1)
            cs = jnp.cumsum(sp, axis=-1)
            keep_sorted = cs - sp < TOP_P
            rows = jnp.arange(probs.shape[0])[:, None]
            mask = jnp.zeros(probs.shape, dtype=bool).at[rows, idx].set(keep_sorted)
            A = probs * mask
            return A / jnp.maximum(A.sum(-1, keepdims=True), 1e-12)
        key = jax.random.key(seed)
        ks = jax.random.split(key, 8)
        N, d, da, steps = (N_NODES, D_IN, D_ATTN, STEPS)
        X = jax.random.normal(ks[0], (N, d), dtype=jnp.float32)
        S = jax.random.uniform(ks[1], (N, N), dtype=jnp.float32)
        W1 = jax.random.normal(ks[2], (da, d), dtype=jnp.float32) / np.sqrt(d)
        W2 = jax.random.normal(ks[3], (da, da), dtype=jnp.float32) / np.sqrt(da)
        W3 = jax.random.normal(ks[4], (da, d), dtype=jnp.float32) / np.sqrt(d)
        U1 = jax.random.normal(ks[5], (steps, d, d), dtype=jnp.float32) / np.sqrt(d)
        U2 = jax.random.normal(ks[6], (steps, d, d), dtype=jnp.float32) / np.sqrt(d)
        ln_g = jnp.ones((d,), dtype=jnp.float32)
        ln_b = jnp.zeros((d,), dtype=jnp.float32)
        return {'X': X, 'S': S, 'W1': W1, 'W2': W2, 'W3': W3, 'U1': U1, 'U2': U2, 'ln_g': ln_g, 'ln_b': ln_b}
    _L0_gnn_all = _L0_gnn_setup()
    _L0_gnn_in = {k: v for k, v in _L0_gnn_all.items() if k in ('W1', 'W2', 'W3', 'U1', 'U2', 'ln_g', 'ln_b')}
    del _L0_gnn_all
    return {'x': x, 'adj': adj, 'L0_gnn_W1': _L0_gnn_in['W1'], 'L0_gnn_W2': _L0_gnn_in['W2'], 'L0_gnn_W3': _L0_gnn_in['W3'], 'L0_gnn_U1': _L0_gnn_in['U1'], 'L0_gnn_U2': _L0_gnn_in['U2'], 'L0_gnn_ln_g': _L0_gnn_in['ln_g'], 'L0_gnn_ln_b': _L0_gnn_in['ln_b']}

def reference(x, adj, L0_gnn_W1, L0_gnn_W2, L0_gnn_W3, L0_gnn_U1, L0_gnn_U2, L0_gnn_ln_g, L0_gnn_ln_b):
    import jax
    import jax.numpy as jnp

    def _L0_gnn_ref(X, S, W1, W2, W3, U1, U2, ln_g, ln_b):
        import jax, jax.numpy as jnp
        import numpy as np
        D_IN = 128
        D_ATTN = 64
        STEPS = 2
        TOP_P = 0.9
        TAU = 1.0
        LN_EPS = 1e-05
        N_NODES = 4096

        def _top_p_attention(X, W1, W2, W3):
            q = X @ W1.T @ W2.T
            k = X @ W3.T
            logits = q @ k.T / TAU
            probs = jax.nn.softmax(logits, axis=-1)
            idx = jnp.argsort(-probs, axis=-1)
            sp = jnp.take_along_axis(probs, idx, axis=-1)
            cs = jnp.cumsum(sp, axis=-1)
            keep_sorted = cs - sp < TOP_P
            rows = jnp.arange(probs.shape[0])[:, None]
            mask = jnp.zeros(probs.shape, dtype=bool).at[rows, idx].set(keep_sorted)
            A = probs * mask
            return A / jnp.maximum(A.sum(-1, keepdims=True), 1e-12)
        N = X.shape[0]
        R = S + jnp.eye(N, dtype=X.dtype)
        R = R / R.sum(-1, keepdims=True)
        Z = jnp.zeros_like(X)
        Xf = X
        Xa = X
        for n in range(STEPS):
            A = _top_p_attention(Xa, W1, W2, W3)
            Xf = R @ Xf
            Xa = A @ Xa
            Z = Z + Xf @ U1[n].T + Xa @ U2[n].T
        h = X + Z
        mu = h.mean(-1, keepdims=True)
        var = jnp.mean((h - mu) ** 2, axis=-1, keepdims=True)
        return (h - mu) / jnp.sqrt(var + LN_EPS) * ln_g + ln_b
    h = jnp.maximum(_layernorm(x, axis=-1), 0.0)
    x = x + _L0_gnn_ref(h, adj, L0_gnn_W1, L0_gnn_W2, L0_gnn_W3, L0_gnn_U1, L0_gnn_U2, L0_gnn_ln_g, L0_gnn_ln_b)
    return x

_drawn_inputs = setup_inputs


def setup_inputs(seed=0):
    import zlib

    import numpy as np

    out = dict(_drawn_inputs(seed))
    spreads = {'L0_gnn_ln_g': (1.0, 0.2), 'L0_gnn_ln_b': (0.0, 0.1)}
    factors = {}
    for name, (base, spread) in spreads.items():
        noise = np.random.default_rng([zlib.crc32(name.encode()), seed]).standard_normal(out[name].shape)
        drawn = base * np.exp(spread * noise) if base else spread * noise
        out[name] = jnp.asarray(drawn.astype(out[name].dtype))
    for name, factor in factors.items():
        out[name] = (out[name] * factor).astype(out[name].dtype)
    return out
```

```python
import concourse.bass as bass
from concourse import mybir
from contextlib import ExitStack


def top_p_graph_mix(nc, x, adj_t, w1_t, w2_tt, w3_tt, u_t, gain, shift, ident_d, out, xf_rows):
    f32, f16, bf16, i32 = mybir.dt.float32, mybir.dt.float16, mybir.dt.bfloat16, mybir.dt.int32
    ALU, ACT, AX = mybir.AluOpType, mybir.ActivationFunctionType, mybir.AxisListType

    P = 128
    N, D = x.shape
    T = N // P
    PAIRS = T // 2
    GROUPS = T // 4
    STEPS = 2
    DE = D + 2
    CH = 1024
    NCH = N // CH
    SJ = 4
    NSC = T // 2 // SJ
    SEG = 256
    NSEG = N // SEG
    ROUNDS = 6
    NTOP = 8 * ROUNDS
    KQ = 10.0
    SHIFT = 13.0
    QS = 256.0
    LS = 1.0 / (QS * QS)
    TAIL = 0.1
    Z10 = 1.2815516
    B10 = 1.7549833
    LN_EPS = 1e-5
    EPS_COLLAPSE = 1.0 + 2.0 ** -22

    with ExitStack() as ctx:
        def sb(name, shape, dt=f32):
            return ctx.enter_context(nc.sbuf_tensor(name, shape, dt))

        def sem(name):
            return ctx.enter_context(nc.semaphore(name))

        e = [[sb(f"e{k}{v}", [P, N]) for v in range(2)] for k in range(2)]
        pm = [sb(f"pm{v}", [P, N]) for v in range(2)]
        hE = sb("hE", [P, T * DE])
        xaE = sb("xaE", [P, T * DE])
        xf = sb("xf", [P, T * D])
        q16 = sb("q16", [P, N], f16)
        k_hi = sb("k_hi", [P, N], f16)
        k_lo = sb("k_lo", [P, N], f16)
        junk = sb("junk", [P, N], bf16)
        s_ring = [sb(f"s_ring{i}", [P, SJ * 512]) for i in range(2)]
        pt = [sb(f"pt{i}", [P, 512]) for i in range(2)]
        out_t = sb("out_t", [P, 512])
        q1s = out_t[0:64, :]
        ident = sb("ident", [P, P])
        ones = sb("ones", [P, NTOP])
        w1 = sb("w1", [P, 64])
        w2 = sb("w2", [64, P])
        w3 = sb("w3", [P, P])
        zf = sb("zf", [P, 512])
        qhi = zf[:].bitcast(f16)[:, 0:512]
        rinv = sb("rinv", [P, T])
        rs = sb("rs", [P, 8])
        mu_row = sb("mu_row", [P, T])
        ks = sb("ks", [P, 1])
        ks16 = sb("ks16", [P, 1], f16)
        st32 = sb("st32", [P, 4 * T])
        mx = sb("mx", [P, 2 * NCH])
        cand = sb("cand", [P, 2 * NSEG * 8])
        top = sb("top", [P, 2 * NTOP])
        pre = sb("pre", [P, 2 * NTOP])
        wn = sb("wn", [P, 2 * NTOP])
        sm = sb("sm", [P, 64])
        flag = sb("flag", [P, 32])
        flag_t = sb("flag_t", [P, 32])
        flag_i = sb("flag_i", [P, 2], i32)
        cst = sb("cst", [P, 8])
        stat = [{n: sb(f"{n}{k}", [P, 2]) for n in
                 ("negm", "mu", "z", "lnr", "f", "g0", "g1", "g2", "nt", "hi", "q", "d",
                  "t0", "t1", "t2", "pw", "l0", "l1", "lo", "a", "b", "c")} for k in range(2)]

        lg = [ctx.enter_context(nc.psum_tensor(f"lg{i}", [P, CH], f32)) for i in range(2)]
        aux = [ctx.enter_context(nc.psum_tensor(f"aux{i}", [P, 512], f32)) for i in range(2)]
        sacc = ctx.enter_context(nc.psum_tensor("sacc", [P, 512], f32))
        pv = ctx.enter_context(nc.psum_tensor("pv", [P, 512], f32))
        RS = 264

        ld_x, ld_w = sem("ld_x"), sem("ld_w")
        consts = sem("consts")
        ln_a, ln_b, ln_c, ln_d = sem("ln_centred"), sem("ln_squares"), sem("ln_var"), sem("ln_rstd")
        h_ready = sem("h_ready")
        su_xt, su_xts, su_q1, su_q1s = sem("su_xt"), sem("su_xts"), sem("su_q1"), sem("su_q1s")
        su_qk, su_split, su_ks, su_mu, su_done = (sem("su_qk"), sem("su_split"), sem("su_ks"),
                                                  sem("su_mu"), sem("su_done"))
        s_loaded = [sem(f"s_loaded{i}") for i in range(2)]
        s_used = [sem(f"s_used{i}") for i in range(2)]
        l_ready, l_evac, neg_ready = sem("l_ready"), sem("l_evac"), sem("neg_ready")
        act_step, pool_t = sem("act_step"), sem("pool_t")
        masked, aux_ready, pt_ready, pt_used = sem("masked"), sem("aux_ready"), sem("pt_ready"), sem("pt_used")
        pv_read = sem("pv_read")
        s_evac, st_ready, s_scaled = sem("s_evac"), sem("st_ready"), sem("s_scaled")
        zf_stored = sem("zf_stored")
        ld_f, fin_tr, fin_ts, fin_z, fin_h, fin_out, stored, fin_free = (sem("ld_f"), sem("fin_tr"), sem("fin_ts"),
                                                               sem("fin_z"), sem("fin_h"), sem("fin_out"), sem("stored"), sem("fin_free"))

        def row_tile(buf, t, w=D):
            return buf[:, bass.ds(t * DE, w)]

        srcE = [hE, xaE]
        src_f = [hE, xf]
        fw = [DE, D]
        fin_src = e[0][1]
        x_fin = e[0][0]
        h2 = e[1][0]
        sq = e[1][1]
        FT = [pm[0][:, 512 * a:512 * (a + 1)] for a in range(4)]
        gsb, bsb = pm[1][:, 0:D], pm[1][:, D:2 * D]
        us = [pm[1][:, D * (2 + a):D * (3 + a)] for a in range(4)]

        def by_tile(buf, n=T, w=D):
            return buf.rearrange("p (t d) -> p t d", d=w)

        block = ctx.enter_context(nc.Block())

        @block.sync
        def _(sp):
            sp.dma_start(by_tile(e[0][0][:]), x.rearrange("(t p) d -> p t d", p=P)).then_inc(ld_x, 16)
            for dst, src in ((w1, w1_t), (w2, w2_tt), (w3, w3_tt), (ident, ident_d)):
                sp.dma_start(dst[:], src).then_inc(ld_w, 16)
            for s in range(STEPS):
                def blocks(g, first=False):
                    for c in range(2 * NSC):
                        i = c % 2
                        if not (first and c < 2):
                            sp.wait_ge(s_used[i], (s * GROUPS + g) * NSC + c // 2)
                        sp.dma_start(s_ring[i][:], adj_t[bass.ds(g, 1), c].rearrange("g p n -> (g p) n")
                                     ).then_inc(s_loaded[i], 16)
                blocks(0, s == 0)
                with sp.Fori(1, GROUPS) as g:
                    blocks(g)
            sp.wait_ge(fin_h, 1)
            sp.wait_ge(zf_stored, 16 * GROUPS)
            sp.dma_start(by_tile(x_fin[:]), x.rearrange("(t p) d -> p t d", p=P)).then_inc(ld_f, 16)
            sp.dma_start(fin_src[:].rearrange("p (g n) -> p g n", n=4 * D), xf_rows.rearrange("g p n -> p g n")).then_inc(ld_f, 16)
            for a in range(4):
                sp.dma_start(us[a], u_t[a]).then_inc(ld_f, 16)
            sp.dma_start(gsb, gain).then_inc(ld_f, 16)
            sp.dma_start(bsb, shift).then_inc(ld_f, 16)
            sp.wait_ge(fin_out, 1)
            sp.dma_start(out.rearrange("(t p) d -> p t d", p=P), by_tile(h2[:])).then_inc(stored, 16)
            sp.wait_ge(stored, 16)

        @block.gpsimd
        def _(pool):
            def op(ins):
                pool.drain()

            g_ = nc.gpsimd
            tt, ts = g_.tensor_tensor, g_.tensor_scalar
            for c, val in enumerate((0.5, 2.718281828459045, -1.0, -0.5)):
                g_.memset(cst[:, 2 * c:2 * c + 2], val)
            pool.drain()
            HALF, EULER, NEG1, NEGH = (cst[:, 2 * c:2 * c + 2] for c in range(4))

            def rstd(n):
                pool.wait_ge(ln_c, n + 1)
                v = st32[:, 2 * T:3 * T]
                op(ts(v, v, 1.0 / D, LN_EPS, ALU.mult, ALU.add))
                tt(v, v, NEGH[:, 0:1].broadcast_to([P, T]), ALU.pow).then_inc(ln_d, 1)

            def pair(s, pr, k):
                gp = s * PAIRS + pr
                m = {n: t_[:] for n, t_ in stat[k].items()}
                z, d, t0, t1, t2, q, a, b, c = (m[n] for n in ("z", "d", "t0", "t1", "t2", "q", "a", "b", "c"))

                def clip(o, src, lo, hi):
                    for v in range(2):
                        c_ = slice(v, v + 1)
                        ts(o[:, c_], src[:, c_], lo[:, c_], hi if isinstance(hi, float) else hi[:, c_], ALU.max, ALU.min)
                    pool.drain()

                pool.wait_ge(act_step, 4 * gp + 1)
                op(tt(a, m["lnr"], m["mu"], ALU.subtract))
                op(ts(a, a, 2.0, 1e-6, ALU.mult, ALU.max))
                op(tt(b, a, HALF, ALU.pow))
                op(ts(m["pw"], b, 1.0 / B10, None, ALU.mult))
                op(tt(a, a, m["mu"], ALU.add))
                op(ts(b, b, -Z10, None, ALU.mult))
                op(tt(a, a, b, ALU.add))
                op(tt(t0, EULER, a, ALU.pow))
                op(ts(d, z, TAIL, None, ALU.mult))
                op(ts(m["lo"], d, 1.01 / N, None, ALU.mult))
                clip(t0, t0, m["lo"], 0.98)
                ts(m["nt"], t0, -1.0, None, ALU.mult).then_inc(pool_t, 1)

                pool.wait_ge(act_step, 4 * gp + 2)
                op(tt(b, d, NEG1, ALU.pow))
                op(ts(a, m["g0"], 0.5, N / 2, ALU.mult, ALU.add))
                op(tt(a, a, t0, ALU.mult))
                op(tt(a, a, m["f"], ALU.add))
                op(tt(m["l0"], z, a, ALU.subtract))
                op(tt(b, b, m["l0"], ALU.mult))
                op(ts(b, b, 1e-6, None, ALU.max))
                op(ts(c, m["pw"], -1.0, None, ALU.mult))
                op(tt(c, b, c, ALU.pow))
                op(ts(c, c, 0.25, 4.0, ALU.max, ALU.min))
                op(tt(t1, t0, c, ALU.mult))
                clip(t1, t1, m["lo"], 0.98)
                ts(m["nt"], t1, -1.0, None, ALU.mult).then_inc(pool_t, 1)
                op(tt(a, m["l0"], NEG1, ALU.pow))
                op(tt(a, a, t0, ALU.mult))
                op(tt(a, a, t0, ALU.mult))
                op(tt(a, a, m["pw"], ALU.mult))
                op(ts(q, a, KQ, 2.0, ALU.mult, ALU.min))

                def secant(ta, tb, tc, la, lb, ga, gb):
                    op(tt(a, ga, gb, ALU.subtract))
                    op(ts(a, a, 0.5, None, ALU.mult))
                    op(tt(b, ta, tb, ALU.add))
                    op(tt(b, b, a, ALU.mult))
                    op(ts(b, b, 0.5, None, ALU.mult))
                    op(tt(lb, la, b, ALU.add))
                    op(tt(b, tb, ta, ALU.subtract))
                    op(tt(a, a, b, ALU.mult))
                    op(tt(b, b, b, ALU.mult))
                    op(ts(c, q, KQ, None, ALU.mult))
                    op(tt(a, a, c, ALU.add))
                    op(tt(c, q, q, ALU.mult))
                    op(tt(b, b, c, ALU.add))
                    op(tt(a, a, NEG1, ALU.pow))
                    op(tt(a, a, b, ALU.mult))
                    op(ts(q, a, KQ, None, ALU.mult))
                    op(tt(c, tb, NEG1, ALU.pow))
                    op(tt(a, a, c, ALU.mult))
                    op(tt(b, d, lb, ALU.subtract))
                    op(tt(a, a, b, ALU.mult))
                    op(tt(tc, tb, a, ALU.add))
                    op(ts(a, tb, 0.6, None, ALU.mult))
                    op(ts(b, tb, 1.6, None, ALU.mult))
                    clip(tc, tc, a, b)
                    clip(tc, tc, m["lo"], 0.98)

                pool.wait_ge(act_step, 4 * gp + 3)
                secant(t0, t1, t2, m["l0"], m["l1"], m["g0"], m["g1"])
                ts(m["nt"], t2, -1.0, None, ALU.mult).then_inc(pool_t, 1)
                pool.wait_ge(act_step, 4 * gp + 4)
                secant(t1, t2, t0, m["l1"], m["l0"], m["g1"], m["g2"])
                op(ts(a, q, SHIFT / KQ, None, ALU.mult))
                op(tt(a, a, t0, ALU.add))
                op(ts(b, m["g2"], 40.0 - N, 2.0, ALU.is_le, ALU.mult))
                for v in range(2):
                    last = ts(m["hi"][:, v:v + 1], a[:, v:v + 1], b[:, v:v + 1], None, ALU.max)
                last.then_inc(pool_t, 1)

            rstd(0)
            for s in range(STEPS):
                def group(g):
                    for u in range(2):
                        pair(s, 2 * g + u, u)
                def store(g):
                    pool.wait_ge(s_scaled, GROUPS + g + 1)
                    pool.dma_start(xf_rows[bass.ds(g, 1)].rearrange("g p n -> (g p) n"), zf[:]).then_inc(zf_stored, 16)

                if s == 0:
                    with pool.Fori(0, GROUPS) as g:
                        group(g)
                else:
                    group(0)
                    with pool.Fori(1, GROUPS) as g:
                        pair(s, 2 * g, 0)
                        store(g - 1)
                        pair(s, 2 * g + 1, 1)
                    store(GROUPS - 1)
            rstd(1)
            rstd(2)

        @block.scalar
        def _(act):
            a_ = nc.scalar.activation

            def squares(n, dst, src):
                act.wait_ge(ln_a, n + 1)
                a_(dst, src, ACT.Square).then_inc(ln_b, 1)

            def setup(s):
                for c in range(N // 512):
                    i = 8 * s + c
                    act.wait_ge(su_xt, i + 1)
                    if c >= 2:
                        act.wait_ge(su_qk, i - 1)
                    a_(pt[c % 2][:], aux[c % 2][:], ACT.Copy).then_inc(su_xts, 1)
                    act.wait_ge(su_q1, i + 1)
                    a_(q1s, sacc[0:64, :], ACT.Copy).then_inc(su_q1s, 1)

            def exponentials(s, pr, k):
                gp = s * PAIRS + pr
                m = stat[k]
                act.wait_ge(neg_ready, gp + 1)
                for v in range(2):
                    a_(e[k][v][:], e[k][v][:], ACT.Exp, bias=m["negm"][:, v:v + 1], scale=LS,
                       accum_out=m["z"][:, v:v + 1])
                act.drain()
                a_(m["lnr"][:], m["z"][:], ACT.Ln, scale=1.0 / N).then_inc(act_step, 1)
                for n, names in enumerate((("f", "g0"), ("g1",), ("g2",))):
                    act.wait_ge(pool_t, 4 * gp + n + 1)
                    for name in names:
                        for v in range(2):
                            last = a_(junk[:], e[k][v][:], ACT.Relu if name == "f" else ACT.Sign,
                                      bias=m["nt"][:, v:v + 1], accum_out=m[name][:, v:v + 1])
                            if not (name == names[-1] and v == 1):
                                act.drain()
                    last.then_inc(act_step, 1)
                    if n < 2:
                        act.drain()
                    else:
                        act.drain()

            def transposed(s, pr):
                gp = s * PAIRS + pr
                for i in range(16):
                    idx = 16 * gp + i
                    act.wait_ge(aux_ready, idx + 1)
                    if s > 0 or i >= 2 or not isinstance(pr, int) or pr > 0:
                        act.wait_ge(pt_used, idx - 1)
                    a_(pt[i % 2][:], aux[i % 2][:], ACT.Copy).then_inc(pt_ready, 1)

            def propagated(s, g):
                act.wait_ge(s_used[1], (s * GROUPS + g + 1) * NSC)
                a_(out_t[:], sacc[:], ACT.Copy).then_inc(s_evac, 1)

            squares(0, pm[0][:], e[0][0][:])
            for s in range(STEPS):
                setup(s)
                exponentials(s, 0, 0)
                exponentials(s, 1, 1)
                transposed(s, 0)
                with act.Fori(1, GROUPS) as g:
                    exponentials(s, 2 * g, 0)
                    propagated(s, g - 1)
                    transposed(s, 2 * g - 1)
                    exponentials(s, 2 * g + 1, 1)
                    transposed(s, 2 * g)
                propagated(s, GROUPS - 1)
                transposed(s, PAIRS - 1)
            squares(1, sq[:], h2[:])
            for g in range(GROUPS):
                for a in range(4):
                    i = 4 * g + a
                    act.wait_ge(fin_tr, i + 1)
                    if g > 0 and a == 0:
                        act.wait_ge(fin_z, g)
                    a_(FT[a], aux[a % 2][:], ACT.Copy).then_inc(fin_ts, 1)
            squares(2, sq[:], h2[:])

        @block.vector
        def _(dve):
            v_ = nc.vector
            B = "p t d -> p t d"

            def op(ins):
                dve.drain()

            def ln_centre(n, buf, w_out=None):
                b3 = by_tile(buf)
                mean = st32[:, 0:T]
                op(v_.tensor_reduce(mean, b3, AX.X, ALU.add))
                op(v_.tensor_scalar(mean, mean, 1.0 / D, None, ALU.mult))
                v_.tensor_tensor(b3, b3, mean.unsqueeze(2).broadcast_to([P, T, D]), ALU.subtract).then_inc(ln_a, 1)

            def ln_var(n, sqb):
                dve.wait_ge(ln_b, n + 1)
                v_.tensor_reduce(st32[:, 2 * T:3 * T], by_tile(sqb), AX.X, ALU.add).then_inc(ln_c, 1)
                dve.wait_ge(ln_d, n + 1)

            rstd_b = st32[:, 2 * T:3 * T].unsqueeze(2).broadcast_to([P, T, D])

            def relu_rows(dst3, src):
                v_.scalar_tensor_tensor(dst3, by_tile(src), 0.0, rstd_b, ALU.max, ALU.mult).then_inc(h_ready, 1)

            def split(s):
                for c in range(N // 512):
                    i = 8 * s + c
                    cols = slice(512 * c, 512 * (c + 1))
                    dve.wait_ge(su_qk, i + 1)
                    qp, kp = lg[c % 2][:, 0:512], lg[c % 2][:, 512:1024]
                    v_.tensor_scalar(qhi, qp, QS, None, ALU.mult)
                    op(v_.tensor_scalar(k_hi[:, cols], kp, QS, None, ALU.mult))
                    v_.tensor_copy(q16[0:64, cols], qhi[0:64, :])
                    v_.scalar_tensor_tensor(q16[64:128, cols], qp[64:128, :], QS, qhi[64:128, :], ALU.mult, ALU.subtract)
                    v_.scalar_tensor_tensor(k_lo[:, cols], kp, QS, k_hi[:, cols], ALU.mult, ALU.subtract
                                            ).then_inc(su_split, 1)
                    dve.drain()
                op(v_.tensor_reduce(ks[:], k_hi[:], AX.X, ALU.add))
                v_.tensor_scalar(ks16[:], ks[:], 1.0 / N, None, ALU.mult).then_inc(su_ks, 1)
                dve.wait_ge(su_mu, s + 1)
                v_.tensor_scalar(mu_row[:], sacc[:, 0:T], LS, None, ALU.mult).then_inc(su_done, 1)
                dve.drain()

            def evacuate(s, pr, k):
                gp = s * PAIRS + pr
                for v in range(2):
                    for c in range(NCH):
                        i = v * NCH + c
                        dve.wait_ge(l_ready, 2 * NCH * gp + i + 1)
                        v_.tensor_scalar(e[k][v][:, CH * c:CH * (c + 1)], lg[i % 2][:], 1.0, None, ALU.mult, ALU.max,
                                         accum_out=mx[:, i:i + 1]).then_inc(l_evac, 1)
                dve.drain()
                m = stat[k]
                op(v_.tensor_reduce(sm[:, 60:62], mx[:].rearrange("p (v c) -> p v c", c=NCH), AX.X, ALU.max))
                op(v_.tensor_scalar(m["negm"][:], sm[:, 60:62], -LS, None, ALU.mult))
                v_.tensor_tensor(m["mu"][:], mu_row[:, bass.ds(2 * pr, 2)], m["negm"][:], ALU.add).then_inc(neg_ready, 1)
                dve.drain()

            LH, V8, TC, OK, DONE, TS, LOB, HIB, HI, A1, A2, A3, PAR = (sm[:, 2 * i:2 * i + 2] for i in range(13))

            def window_masks(k):
                for v in range(2):
                    v_.scalar_tensor_tensor(pm[v][:], e[k][v][:], HI[:, v:v + 1], e[k][v][:], ALU.is_lt, ALU.mult,
                                            accum_out=LH[:, v:v + 1])
                dve.drain()

            def window_search(k):
                d = stat[k]["d"]
                c3 = cand[:].rearrange("p (v s m) -> p v s m", v=2, m=8)
                for v in range(2):
                    for sg in range(NSEG):
                        v_.max(c3[:, v, sg, :], pm[v][:, SEG * sg:SEG * (sg + 1)])
                dve.drain()
                v_.tensor_reduce(V8, c3[:, :, :, 7], AX.X, ALU.max)
                for r in range(ROUNDS):
                    for v in range(2):
                        v_.max(top[:, NTOP * v + 8 * r:NTOP * v + 8 * (r + 1)], cand[:, NSEG * 8 * v:NSEG * 8 * (v + 1)])
                    dve.drain()
                    if r < ROUNDS - 1:
                        for v in range(2):
                            cv = cand[:, NSEG * 8 * v:NSEG * 8 * (v + 1)]
                            v_.match_replace(cv, top[:, NTOP * v + 8 * r:NTOP * v + 8 * (r + 1)], cv, -1.0)
                        dve.drain()
                for v in range(2):
                    c = slice(NTOP * v, NTOP * (v + 1))
                    v_.tensor_tensor_scan(pre[:, c], ones[:], top[:, c], LH[:, v:v + 1], ALU.mult, ALU.subtract)
                dve.drain()
                for v in range(2):
                    c = slice(NTOP * v, NTOP * (v + 1))
                    v_.scalar_tensor_tensor(wn[:, c], pre[:, c], d[:, v:v + 1], top[:, c], ALU.is_le, ALU.mult)
                v_.tensor_tensor(A1, LH, d[:], ALU.is_gt)
                dve.drain()
                op(v_.tensor_reduce(TC, wn[:].rearrange("p (v c) -> p v c", v=2), AX.X, ALU.max))
                op(v_.tensor_tensor(A2, TC, V8, ALU.is_gt))
                op(v_.tensor_tensor(OK, A1, A2, ALU.mult))

            def open_rows(reg):
                op(v_.tensor_tensor(A2, DONE[:, 0:1].broadcast_to([P, 2]), DONE, ALU.mult))
                op(v_.tensor_scalar(flag[:, 0:1], A2[:, 1:2], 0.5, None, ALU.is_lt))
                op(v_.transpose(flag_t[:], flag[:]))
                op(v_.tensor_reduce(flag_t[:, 0:1], flag_t[:, 0:32], AX.X, ALU.max))
                for q in range(1, 4):
                    v_.tensor_copy(flag_t[0:1, q:q + 1], flag_t[32 * q:32 * q + 1, 0:1])
                dve.drain()
                op(v_.tensor_reduce(flag_i[0:1, 0:1], flag_t[0:1, 0:4], AX.X, ALU.max))
                dve.load(reg, flag_i[0:1, 0:1])

            def retry(k, reg):
                m = stat[k]
                d, q = m["d"][:], m["q"][:]
                op(v_.tensor_tensor(A1, LH, d, ALU.is_gt))
                op(v_.tensor_scalar(A2, A1, -4.0, 4.0, ALU.mult, ALU.add))
                op(v_.tensor_tensor(A2, A2, HI, ALU.add))
                op(v_.tensor_tensor(HIB, HIB, A2, ALU.min))
                op(v_.tensor_scalar(A1, A1, -1.0, 1.0, ALU.mult, ALU.add))
                op(v_.tensor_tensor(A1, A1, HI, ALU.mult))
                op(v_.tensor_tensor(LOB, LOB, A1, ALU.max))
                op(v_.reciprocal(A1, HI))
                op(v_.tensor_tensor(A2, d, LH, ALU.subtract))
                op(v_.tensor_tensor(A1, A1, A2, ALU.mult))
                op(v_.tensor_scalar(A1, A1, 1.0 / KQ, SHIFT / KQ, ALU.mult, ALU.add))
                op(v_.tensor_tensor(A1, A1, q, ALU.mult))
                op(v_.tensor_tensor(A1, A1, HI, ALU.add))
                op(v_.tensor_tensor(A2, LOB, HIB, ALU.add))
                op(v_.tensor_scalar(A2, A2, 0.5, None, ALU.mult))
                op(v_.tensor_scalar(PAR, PAR, -1.0, 1.0, ALU.mult, ALU.add))
                op(v_.tensor_tensor(A3, A1, LOB, ALU.is_gt))
                op(v_.tensor_tensor(A3, A3, PAR, ALU.mult))
                op(v_.tensor_tensor(OK, A1, HIB, ALU.is_lt))
                op(v_.tensor_tensor(A3, A3, OK, ALU.mult))
                op(v_.tensor_tensor(A1, A1, A2, ALU.subtract))
                op(v_.tensor_tensor(A1, A1, A3, ALU.mult))
                op(v_.tensor_tensor(HI, A1, A2, ALU.add))
                window_masks(k)
                window_search(k)
                settle()
                op(v_.scalar_tensor_tensor(A1, LOB, EPS_COLLAPSE, HIB, ALU.mult, ALU.is_ge))
                op(v_.tensor_scalar(A2, DONE, -1.0, 1.0, ALU.mult, ALU.add))
                op(v_.tensor_tensor(A1, A1, A2, ALU.mult))
                op(v_.tensor_tensor(A2, A1, LOB, ALU.mult))
                op(v_.tensor_tensor(TS, TS, A2, ALU.add))
                op(v_.tensor_tensor(DONE, DONE, A1, ALU.add))
                open_rows(reg)

            def settle():
                op(v_.tensor_scalar(A1, DONE, -1.0, 1.0, ALU.mult, ALU.add))
                op(v_.tensor_tensor(A1, A1, OK, ALU.mult))
                op(v_.tensor_tensor(A2, A1, TC, ALU.mult))
                op(v_.tensor_tensor(TS, TS, A2, ALU.add))
                op(v_.tensor_tensor(DONE, DONE, A1, ALU.add))

            def attended(s, pr, u):
                gp = s * PAIRS + pr
                dve.wait_ge(pt_used, 16 * gp + 16)
                dst = xaE if s == 0 else hE
                for v in range(2):
                    v_.reciprocal(sm[:, 40 + v:41 + v], pv[:, DE * v + D:DE * v + D + 1])
                if s == 0:
                    if u == 0:
                        v_.tensor_scalar(rs[:, 0:4], pv[:, RS:RS + 4], 1.0, None, ALU.add)
                    else:
                        v_.tensor_tensor(rs[:, 4:8], rs[:, 0:4], pv[:, RS:RS + 4], ALU.add)
                dve.drain()
                if s == 0 and u == 1:
                    v_.reciprocal(rinv[:, bass.ds((pr - 1) * 2, 4)], rs[:, 4:8])
                for v in range(2):
                    last = v_.tensor_scalar(row_tile(dst, 2 * pr + v), pv[:, DE * v:DE * v + D], sm[:, 40 + v:41 + v],
                                            None, ALU.mult)
                last.then_inc(pv_read, 1)
                dve.drain()

            def scaled(s, g):
                dve.wait_ge(st_ready, s * GROUPS + g + 1)
                w = fw[s]
                prev = src_f[s][:, bass.ds(g * (4 * w), 4 * w)].rearrange("p (t d) -> p t d", d=w)[:, :, 0:D]
                if s == 1:
                    if not isinstance(g, int) or g > 0:
                        dve.wait_ge(zf_stored, 16 * g)
                dst = xf[:, bass.ds(g * (4 * D), 4 * D)] if s == 0 else zf[:]
                z3 = by_tile(sacc[:], 4)
                t3 = by_tile(zf[:], 4)
                op(v_.tensor_tensor(t3, z3, prev, ALU.add))
                v_.tensor_tensor(by_tile(dst, 4), t3, rinv[:, bass.ds(g * 4, 4)].unsqueeze(2).broadcast_to([P, 4, D]),
                                 ALU.mult).then_inc(s_scaled, 1)
                dve.drain()

            def finish(s, pr, k, reg, between):
                gp = s * PAIRS + pr
                m = stat[k]
                dve.wait_ge(pool_t, 4 * gp + 4)
                v_.tensor_copy(HI, m["hi"][:])
                v_.memset(DONE, 0.0)
                v_.memset(TS, 0.0)
                v_.memset(PAR, 0.0)
                v_.tensor_scalar(LOB, m["d"][:], 0.5 / N, None, ALU.mult)
                v_.memset(HIB, 2.5)
                dve.drain()
                if s > 0 or not isinstance(pr, int) or pr > 0:
                    dve.wait_ge(aux_ready, 16 * gp)
                window_masks(k)
                between()
                window_search(k)
                settle()
                open_rows(reg)
                with dve.While(lambda: dve.snap(reg) > 0):
                    retry(k, reg)
                for v in range(2):
                    v_.scalar_tensor_tensor(pm[v][:], e[k][v][:], TS[:, v:v + 1], e[k][v][:], ALU.is_ge, ALU.mult
                                            ).then_inc(masked, 1)
                dve.drain()

            reg = dve.alloc_register("open_rows")
            v_.memset(flag[:], 0.0)
            v_.memset(ones[:], 1.0)
            for buf in (hE, xaE):
                last = v_.memset(by_tile(buf[:], T, DE)[:, :, D:DE], 1.0)
            last.then_inc(consts, 1)
            dve.wait_ge(ld_x, 16)
            ln_centre(0, e[0][0][:])
            ln_var(0, pm[0][:])
            relu_rows(by_tile(hE[:], T, DE)[:, :, 0:D], e[0][0][:])
            dve.drain()
            for s in range(STEPS):
                split(s)
                evacuate(s, 0, 0)
                evacuate(s, 1, 1)

                def group(g, first=False, last=False):
                    for u in range(2):
                        pr = 2 * g + u

                        def between():
                            if not (first and u == 0):
                                attended(s, pr - 1, 1 - u)
                            if u == 0 and not first:
                                scaled(s, g - 1)
                        finish(s, pr, u, reg, between)
                        if not last:
                            evacuate(s, pr + 2, u)
                group(0, first=True)
                with dve.Fori(1, GROUPS - 1) as g:
                    group(g)
                group(GROUPS - 1, last=True)
                attended(s, PAIRS - 1, 1)
                scaled(s, GROUPS - 1)
            v_.memset(sm[:, 42:43], 0.0).then_inc(fin_h, 1)
            dve.wait_ge(ld_f, 16 * 8)
            v_.tensor_copy(h2[:], x_fin[:])
            dve.drain()
            ln_centre(1, h2[:])
            dve.wait_ge(ln_b, 2)
            v_.tensor_reduce(st32[:, 2 * T:3 * T], by_tile(sq[:]), AX.X, ALU.add).then_inc(ln_c, 1)
            dve.wait_ge(ln_d, 2)
            op(v_.scalar_tensor_tensor(by_tile(h2[:]), by_tile(h2[:]), 0.0, rstd_b, ALU.max, ALU.mult))
            for g in range(GROUPS):
                dve.wait_ge(fin_z, g + 1)
                c = slice(512 * g, 512 * (g + 1))
                v_.tensor_tensor(h2[:, c], h2[:, c], lg[g % 2][:, 0:512], ALU.add).then_inc(fin_free, 1)
            dve.drain()
            ln_centre(2, h2[:])
            dve.wait_ge(ln_b, 3)
            v_.tensor_reduce(st32[:, 2 * T:3 * T], by_tile(sq[:]), AX.X, ALU.add).then_inc(ln_c, 1)
            dve.wait_ge(ln_d, 3)
            op(v_.tensor_tensor(by_tile(h2[:]), by_tile(h2[:]), rstd_b, ALU.mult))
            op(v_.tensor_tensor(by_tile(h2[:]), by_tile(h2[:]), gsb.unsqueeze(1).broadcast_to([P, T, D]), ALU.mult))
            op(v_.tensor_tensor(by_tile(h2[:]), by_tile(h2[:]), bsb.unsqueeze(1).broadcast_to([P, T, D]), ALU.add))
            v_.tensor_tensor(h2[:], h2[:], x_fin[:], ALU.add).then_inc(fin_out, 1)

        @block.tensor
        def _(pe):
            mm, tr = nc.tensor.matmul, nc.tensor.transpose

            def setup(s):
                if s == 0:
                    pe.wait_ge(ld_w, 64)
                    pe.wait_ge(consts, 1)
                    pe.wait_ge(h_ready, 1)
                else:
                    pe.wait_ge(pv_read, PAIRS)
                    pe.wait_ge(s_scaled, GROUPS)
                for c in range(N // 512):
                    i = 8 * s + c
                    if c >= 2:
                        pe.wait_ge(su_xts, i - 1)
                    for m in range(4):
                        last = tr(aux[c % 2][:, P * m:P * (m + 1)], row_tile(srcE[s], 4 * c + m), ident[:])
                    last.then_inc(su_xt, 1)
                    pe.wait_ge(su_xts, i + 1)
                    if i > 0:
                        pe.wait_ge(su_q1s, i)
                    mm(sacc[0:64, :], w1[:], pt[c % 2][:], start=True, stop=True).then_inc(su_q1, 1)
                    pe.wait_ge(su_q1s, i + 1)
                    if c >= 2:
                        pe.wait_ge(su_split, i - 1)
                    mm(lg[c % 2][:, 0:512], w2[:], q1s, start=True, stop=True)
                    mm(lg[c % 2][:, 512:1024], w3[:], pt[c % 2][:], start=True, stop=True).then_inc(su_qk, 1)
                pe.wait_ge(su_ks, s + 1)
                for t in range(T):
                    last = mm(sacc[:, t:t + 1], q16[:, P * t:P * (t + 1)], ks16[:], start=True, stop=True)
                last.then_inc(su_mu, 1)
                pe.wait_ge(su_done, s + 1)

            def logits(s, pr, i):
                v, c = divmod(i, NCH)
                idx = 2 * NCH * (s * PAIRS + pr) + i
                if s > 0 or i >= 2 or not isinstance(pr, int) or pr > 0:
                    pe.wait_ge(l_evac, idx - 1)
                q = q16[:, bass.ds((2 * pr + v) * P, P)]
                for h in range(2):
                    o = lg[i % 2][:, 512 * h:512 * (h + 1)]
                    cols = slice(CH * c + 512 * h, CH * c + 512 * (h + 1))
                    mm(o, q, k_hi[:, cols], start=True, stop=False)
                    last = mm(o, q, k_lo[:, cols], start=False, stop=True)
                last.then_inc(l_ready, 1)

            def propagate(s, g, u):
                if u == 0 and (not isinstance(g, int) or g > 0):
                    pe.wait_ge(s_scaled, s * GROUPS + g)
                for c in range(NSC):
                    cc = NSC * u + c
                    i = cc % 2
                    pe.wait_ge(s_loaded[i], 16 * ((s * GROUPS + g) * NSC + cc // 2 + 1))
                    for j in range(SJ):
                        n = cc * SJ + j
                        last = mm(sacc[:], src_f[s][:, n * fw[s]:n * fw[s] + D], s_ring[i][:, 512 * j:512 * (j + 1)],
                                  start=n == 0, stop=n == T - 1)
                        if s == 0:
                            for m in range(4):
                                last = mm(pv[:, RS + m:RS + m + 1], s_ring[i][:, 512 * j + P * m:512 * j + P * (m + 1)],
                                          ones[:, 0:1], start=c == 0 and j == 0 and m == 0,
                                          stop=c == NSC - 1 and j == SJ - 1, skip_group_check=True)
                    last.then_inc(s_used[i], 1)

            def attend(s, pr, v, q):
                idx = 16 * (s * PAIRS + pr) + 8 * v + q
                pe.wait_ge(pt_ready, idx + 1)
                for j in range(4):
                    t = 4 * q + j
                    last = mm(pv[:, DE * v:DE * v + D + 1], pt[q % 2][:, P * j:P * (j + 1)],
                              row_tile(srcE[s], t, D + 1), start=t == 0, stop=t == T - 1)
                last.then_inc(pt_used, 1)

            def iteration(s, g, u, last_group=False):
                pr = 2 * g + u
                gp = s * PAIRS + pr
                started = s > 0 or u > 0 or not isinstance(g, int) or g > 0
                if not last_group:
                    logits(s, pr + 2, 0)
                    logits(s, pr + 2, 1)
                if s == 0 and started:
                    pe.wait_ge(pv_read, gp)
                propagate(s, g, u)
                if s > 0:
                    pe.wait_ge(pv_read, gp)
                for n in range(16):
                    v, q = divmod(n, 8)
                    if q == 0:
                        pe.wait_ge(masked, 2 * gp + v + 1)
                    if started or n >= 2:
                        pe.wait_ge(pt_ready, 16 * gp + n - 1)
                    for m in range(4):
                        t = 4 * q + m
                        last = tr(aux[q % 2][:, P * m:P * (m + 1)], pm[v][:, P * t:P * (t + 1)], ident[:])
                    last.then_inc(aux_ready, 1)
                    if n > 0:
                        attend(s, pr, *divmod(n - 1, 8))
                    if v == 1 and q < 6 and not last_group:
                        logits(s, pr + 2, 2 + q)
                attend(s, pr, 1, 7)
                if u == 1:
                    pe.wait_ge(s_evac, s * GROUPS + g + 1)
                    for m in range(4):
                        last = tr(sacc[:, P * m:P * (m + 1)], out_t[:, P * m:P * (m + 1)], ident[:])
                    last.then_inc(st_ready, 1)

            for s in range(STEPS):
                setup(s)
                for pr in range(2):
                    for i in range(2 * NCH):
                        logits(s, pr, i)
                for u in range(2):
                    iteration(s, 0, u)
                with pe.Fori(1, GROUPS - 1) as g:
                    for u in range(2):
                        iteration(s, g, u)
                for u in range(2):
                    iteration(s, GROUPS - 1, u, last_group=True)
            pe.wait_ge(ld_f, 16 * 8)
            rows = ((xf, D), (xaE, DE), (fin_src, D), (hE, DE))
            for g in range(GROUPS):
                for a, (src, w) in enumerate(rows):
                    i = 4 * g + a
                    if i >= 2:
                        pe.wait_ge(fin_ts, i - 1)
                    for m in range(4):
                        t = 4 * g + m
                        last = tr(aux[a % 2][:, P * m:P * (m + 1)], src[:, w * t:w * t + D], ident[:])
                    last.then_inc(fin_tr, 1)
                pe.wait_ge(fin_ts, 4 * g + 4)
                if g >= 2:
                    pe.wait_ge(fin_free, g - 1)
                for m in range(4):
                    for a in range(4):
                        last = mm(lg[g % 2][:, P * m:P * (m + 1)], FT[a][:, P * m:P * (m + 1)], us[a],
                                  start=a == 0, stop=a == 3)
                last.then_inc(fin_z, 1)

    return nc


_IN = ["x", "adj_t", "w1_t", "w2_tt", "w3_tt", "u_t", "gain", "shift", "ident"]


def kernel(x, adj, L0_gnn_W1, L0_gnn_W2, L0_gnn_W3, L0_gnn_U1, L0_gnn_U2, L0_gnn_ln_g, L0_gnn_ln_b):
    import numpy as np
    import concourse.bacc as bacc
    from concourse import mybir
    from concourse.bass_utils import run_bass_kernel_spmd

    c = np.ascontiguousarray
    x, adj, w1, w2, w3, u1, u2 = (np.asarray(a) for a in (x, adj, L0_gnn_W1, L0_gnn_W2, L0_gnn_W3, L0_gnn_U1, L0_gnn_U2))
    n = x.shape[0]
    adj_t = c(adj.reshape(n // 512, 512, n // 512, 4, 128).transpose(0, 2, 4, 3, 1)).reshape(n // 512, n // 512, 128, 2048)
    arrays = {
        "x": c(x), "adj_t": adj_t, "w1_t": c(w1.T),
        "w2_tt": c(np.concatenate([w2.T, w2.T], 1)), "w3_tt": c(np.concatenate([w3.T, w3.T], 1)),
        "u_t": c(np.stack([u1[0].T, u2[0].T, u1[1].T, u2[1].T])),
        "gain": c(np.broadcast_to(np.asarray(L0_gnn_ln_g), (128, x.shape[1]))),
        "shift": c(np.broadcast_to(np.asarray(L0_gnn_ln_b), (128, x.shape[1]))),
        "ident": np.eye(128, dtype=np.float32),
    }
    nc = bacc.Bacc("TRN2", target_bir_lowering=False, num_devices=1)
    args = [nc.dram_tensor(f"in_{k}", arrays[k].shape, mybir.dt.from_np(arrays[k].dtype), kind="ExternalInput").ap()
            for k in _IN]
    out = nc.dram_tensor("out_0", x.shape, mybir.dt.float32, kind="ExternalOutput").ap()
    rows = nc.dram_tensor("xf_rows", (n // 512, 128, 512), mybir.dt.float32, kind="Internal").ap()
    top_p_graph_mix(nc, *args, out, rows)
    r = run_bass_kernel_spmd(nc, [{f"in_{k}": arrays[k] for k in _IN}], core_ids=[0])
    return r.results[0]["out_0"]
```

```python
import concourse.bass as bass
from concourse import mybir
from contextlib import ExitStack


def top_p_graph_mix(nc, x, adj_t, w1_t, w2_tt, w3_tt, u_t, gain, shift, ident_d, out, xf_rows):
    f32, f16, bf16, i32 = mybir.dt.float32, mybir.dt.float16, mybir.dt.bfloat16, mybir.dt.int32
    ALU, ACT, AX = mybir.AluOpType, mybir.ActivationFunctionType, mybir.AxisListType

    P = 128
    N, D = x.shape
    T = N // P
    PAIRS = T // 2
    GROUPS = T // 4
    STEPS = 2
    DE = D + 2
    CH = 1024
    NCH = N // CH
    SJ = 2
    NSC = T // 2 // SJ
    SEG = 256
    NSEG = N // SEG
    WC = 1024
    NWC = N // WC
    ROUNDS = 6
    NTOP = 8 * ROUNDS
    KQ = 10.0
    SHIFT = 13.0
    QS = 256.0
    LS = 1.0 / (QS * QS)
    TAIL = 0.1
    Z10 = 1.2815516
    B10 = 1.7549833
    LN_EPS = 1e-5
    LNR = 2.0 ** -8
    EPS_COLLAPSE = 1.0 + 2.0 ** -22

    with ExitStack() as ctx:
        def sb(name, shape, dt=f32):
            return ctx.enter_context(nc.sbuf_tensor(name, shape, dt))

        def sem(name):
            return ctx.enter_context(nc.semaphore(name))

        e = [[sb(f"e{k}{v}", [P, N]) for v in range(2)] for k in range(2)]
        pm = [sb(f"pm{v}", [P, N]) for v in range(2)]
        hE = sb("hE", [P, T * DE])
        xaE = sb("xaE", [P, T * DE])
        xf = sb("xf", [P, T * D])
        q16 = sb("q16", [P, N], f16)
        k_hi = sb("k_hi", [P, N], f16)
        k_lo = sb("k_lo", [P, N], f16)
        junk = sb("junk", [P, N], bf16)
        win = [sb(f"win{i}", [P, WC]) for i in range(2)]
        s_ring = [sb(f"s_ring{i}", [P, SJ * 512]) for i in range(2)]
        pt = [sb(f"pt{i}", [P, 512]) for i in range(2)]
        q1s_b = sb("q1s", [P, 512])
        q1s = q1s_b[0:64, :]
        half = q1s_b[:, 0:D + 1]
        ident = sb("ident", [P, P])
        ones = sb("ones", [P, NTOP])
        w1 = sb("w1", [P, 64])
        w2 = sb("w2", [64, P])
        w3 = sb("w3", [P, P])
        zf = sb("zf", [P, 512])
        qhi = zf[:].bitcast(f16)[:, 0:512]
        rinv = sb("rinv", [P, T])
        rs = sb("rs", [P, 8])
        mu_row = sb("mu_row", [P, T])
        ks = sb("ks", [P, 1])
        ks16 = sb("ks16", [P, 1], f16)
        st32 = sb("st32", [P, 4 * T])
        mx = sb("mx", [P, 2 * NCH])
        lh = sb("lh", [P, 2 * NWC])
        cand = sb("cand", [P, 2 * NSEG * 8])
        top = sb("top", [P, 2 * NTOP])
        pre = sb("pre", [P, 2 * NTOP])
        wn = sb("wn", [P, 2 * NTOP])
        sm = sb("sm", [P, 64])
        flag = sb("flag", [P, 32])
        flag_t = sb("flag_t", [P, 32])
        flag_i = sb("flag_i", [P, 2], i32)
        cst = sb("cst", [P, 16])
        STATS = ("negm", "mu", "z", "f", "g0", "g1", "g2", "nt", "hi", "q", "d",
                  "t0", "t1", "t2", "pw", "npw", "l0", "l1", "lo", "tlo", "thi", "w", "bh", "kq", "bb", "it", "a", "b", "c")
        stats = [sb(f"stats{k}", [P, 2 * len(STATS)]) for k in range(2)]
        stat = [{n: stats[k][:, 2 * i:2 * i + 2] for i, n in enumerate(STATS)} for k in range(2)]

        lg = [ctx.enter_context(nc.psum_tensor(f"lg{i}", [P, CH], f32)) for i in range(2)]
        aux = [ctx.enter_context(nc.psum_tensor(f"aux{i}", [P, 512], f32)) for i in range(2)]
        sacc = ctx.enter_context(nc.psum_tensor("sacc", [P, 512], f32))
        pv = ctx.enter_context(nc.psum_tensor("pv", [P, 512], f32))
        RS = 264

        ld_x, ld_w = sem("ld_x"), sem("ld_w")
        consts = sem("consts")
        ln_a, ln_b, ln_c, ln_d = sem("ln_centred"), sem("ln_squares"), sem("ln_var"), sem("ln_rstd")
        h_ready = sem("h_ready")
        su_xt, su_xts, su_q1, su_q1s = sem("su_xt"), sem("su_xts"), sem("su_q1"), sem("su_q1s")
        su_qk, su_split, su_ks, su_mu, su_done = (sem("su_qk"), sem("su_split"), sem("su_ks"),
                                                  sem("su_mu"), sem("su_done"))
        s_loaded = [sem(f"s_loaded{i}") for i in range(2)]
        s_used = [sem(f"s_used{i}") for i in range(2)]
        l_ready, l_evac, neg_ready = sem("l_ready"), sem("l_evac"), sem("neg_ready")
        act_step, pool_t = sem("act_step"), sem("pool_t")
        masked, aux_ready, pt_ready, pt_used = sem("masked"), sem("aux_ready"), sem("pt_ready"), sem("pt_used")
        pv_read = sem("pv_read")
        s_scaled = sem("s_scaled")
        zf_stored = sem("zf_stored")
        ld_f, fin_tr, fin_ts, fin_z, fin_h, fin_out, stored, fin_free = (sem("ld_f"), sem("fin_tr"), sem("fin_ts"),
                                                               sem("fin_z"), sem("fin_h"), sem("fin_out"), sem("stored"), sem("fin_free"))

        def row_tile(buf, t, w=D):
            return buf[:, bass.ds(t * DE, w)]

        srcE = [hE, xaE]
        src_f = [hE, xf]
        fw = [DE, D]
        fin_src = e[0][1]
        x_fin = e[0][0]
        h2 = e[1][0]
        sq = e[1][1]
        FT = [pm[0][:, 512 * a:512 * (a + 1)] for a in range(4)]
        gsb, bsb = pm[1][:, 0:D], pm[1][:, D:2 * D]
        us = [pm[1][:, D * (2 + a):D * (3 + a)] for a in range(4)]

        def prop(m, w=D):
            return sacc[:, DE * m:DE * m + w] if m < 3 else pv[:, RS:RS + w]

        def by_tile(buf, n=T, w=D):
            return buf.rearrange("p (t d) -> p t d", d=w)

        def thresholds_before(s, pr):
            return 4 * (s * PAIRS + pr)

        block = ctx.enter_context(nc.Block())

        @block.sync
        def _(sp):
            sp.dma_start(by_tile(e[0][0][:]), x.rearrange("(t p) d -> p t d", p=P)).then_inc(ld_x, 16)
            for dst, src in ((w1, w1_t), (w2, w2_tt), (w3, w3_tt), (ident, ident_d)):
                sp.dma_start(dst[:], src).then_inc(ld_w, 16)
            for s in range(STEPS):
                def store(g):
                    sp.wait_ge(s_scaled, GROUPS + g + 1)
                    sp.dma_start(xf_rows[bass.ds(g, 1)].rearrange("g p n -> (g p) n"), zf[:]).then_inc(zf_stored, 16)

                def blocks(g, first=False):
                    for c in range(2 * NSC):
                        i = c % 2
                        if c == 2 and s == 1 and not (isinstance(g, int) and g == 0):
                            store(g - 1)
                        if not (first and c < 2):
                            sp.wait_ge(s_used[i], (s * GROUPS + g) * NSC + c // 2)
                        sp.dma_start(s_ring[i][:], adj_t[bass.ds(g, 1), c].rearrange("g p n -> (g p) n")
                                     ).then_inc(s_loaded[i], 16)
                blocks(0, s == 0)
                with sp.Fori(1, GROUPS) as g:
                    blocks(g)
                if s == 1:
                    store(GROUPS - 1)
            sp.wait_ge(fin_h, 1)
            sp.wait_ge(zf_stored, 16 * GROUPS)
            sp.dma_start(by_tile(x_fin[:]), x.rearrange("(t p) d -> p t d", p=P)).then_inc(ld_f, 16)
            sp.dma_start(fin_src[:].rearrange("p (g n) -> p g n", n=4 * D), xf_rows.rearrange("g p n -> p g n")).then_inc(ld_f, 16)
            for a in range(4):
                sp.dma_start(us[a], u_t[a]).then_inc(ld_f, 16)
            sp.dma_start(gsb, gain).then_inc(ld_f, 16)
            sp.dma_start(bsb, shift).then_inc(ld_f, 16)
            sp.wait_ge(fin_out, 1)
            sp.dma_start(out.rearrange("(t p) d -> p t d", p=P), by_tile(h2[:])).then_inc(stored, 16)
            sp.wait_ge(stored, 16)

        @block.gpsimd
        def _(pool):
            def op(ins):
                pool.drain()

            g_ = nc.gpsimd
            tt, ts = g_.tensor_tensor, g_.tensor_scalar
            for c, val in enumerate((0.5, 2.718281828459045, -1.0, -0.5, 1.0 / N, LNR, -LNR, float(N))):
                g_.memset(cst[:, 2 * c:2 * c + 2], val)
            pool.drain()
            HALF, EULER, NEG1, NEGH, R_N, POSR, NEGR, NUM = (cst[:, 2 * c:2 * c + 2] for c in range(8))

            def rstd(n):
                pool.wait_ge(ln_c, n + 1)
                v = st32[:, 2 * T:3 * T]
                op(ts(v, v, 1.0 / D, LN_EPS, ALU.mult, ALU.add))
                tt(v, v, NEGH[:, 0:1].broadcast_to([P, T]), ALU.pow).then_inc(ln_d, 1)

            def pair(s, pr, k):
                base = thresholds_before(s, pr)
                m = {n: t_[:] for n, t_ in stat[k].items()}
                z, d, t0, t1, t2, q, a, b, c = (m[n] for n in ("z", "d", "t0", "t1", "t2", "q", "a", "b", "c"))

                def bounds(t, down, up):
                    for v in range(2):
                        c_ = slice(v, v + 1)
                        ts(m["tlo"][:, c_], t[:, c_], down, m["lo"][:, c_], ALU.mult, ALU.max)
                    op(ts(m["thi"], t, up, 0.98, ALU.mult, ALU.min))

                def clip(o, src, lo, hi):
                    for v in range(2):
                        c_ = slice(v, v + 1)
                        ts(o[:, c_], src[:, c_], lo[:, c_], hi if isinstance(hi, float) else hi[:, c_], ALU.max, ALU.min)
                    pool.drain()

                pool.wait_ge(act_step, base + 1)
                op(tt(a, z, R_N, ALU.mult))
                op(tt(b, a, NEGR, ALU.pow))
                op(tt(a, a, POSR, ALU.pow))
                op(tt(a, a, b, ALU.subtract))
                op(ts(b, m["mu"], 2.0 * LNR, None, ALU.mult))
                op(tt(a, a, b, ALU.subtract))
                op(ts(a, a, 1.0 / LNR, 1e-6, ALU.mult, ALU.max))
                op(tt(b, a, HALF, ALU.pow))
                op(tt(a, a, m["mu"], ALU.add))
                op(ts(c, b, -Z10, None, ALU.mult))
                op(tt(a, a, c, ALU.add))
                op(tt(t0, EULER, a, ALU.pow))
                op(ts(m["lo"], z, 1.01 * TAIL / N, None, ALU.mult))
                clip(t0, t0, m["lo"], 0.98)
                ts(m["nt"], t0, -1.0, None, ALU.mult).then_inc(pool_t, 1)
                bounds(t0, 0.25, 4.0)
                op(ts(d, z, TAIL, None, ALU.mult))
                op(tt(c, d, NEG1, ALU.pow))
                op(ts(m["pw"], b, 1.0 / B10, None, ALU.mult))
                op(ts(m["npw"], b, -1.0 / B10, None, ALU.mult))
                op(tt(q, t0, t0, ALU.mult))
                op(tt(q, q, m["pw"], ALU.mult))

                pool.wait_ge(act_step, base + 2)
                op(tt(b, m["g0"], NUM, ALU.add))
                op(tt(b, b, t0, ALU.mult))
                op(ts(b, b, 0.5, None, ALU.mult))
                op(tt(b, b, m["f"], ALU.add))
                op(tt(m["l0"], z, b, ALU.subtract))
                op(tt(b, c, m["l0"], ALU.mult))
                op(ts(b, b, 1e-6, None, ALU.max))
                op(tt(c, b, m["npw"], ALU.pow))
                op(tt(t1, t0, c, ALU.mult))
                clip(t1, t1, m["tlo"], m["thi"])
                ts(m["nt"], t1, -1.0, None, ALU.mult).then_inc(pool_t, 1)
                op(ts(a, m["l0"], 1e-9, None, ALU.max))
                op(tt(a, a, NEG1, ALU.pow))
                op(tt(a, a, q, ALU.mult))
                op(ts(q, a, KQ, 2.0, ALU.mult, ALU.min))

                def before_count(ta, tb):
                    op(tt(m["w"], ta, tb, ALU.add))
                    op(ts(m["w"], m["w"], 0.25, None, ALU.mult))
                    op(tt(b, tb, ta, ALU.subtract))
                    op(ts(m["bh"], b, 0.5, None, ALU.mult))
                    op(ts(m["kq"], q, KQ, None, ALU.mult))
                    op(tt(b, b, b, ALU.mult))
                    op(tt(c, q, q, ALU.mult))
                    op(tt(m["bb"], b, c, ALU.add))
                    op(tt(m["it"], tb, NEG1, ALU.pow))
                    bounds(tb, 0.6, 1.6)

                def secant(tb, tc, la, lb, ga, gb):
                    op(tt(a, ga, gb, ALU.subtract))
                    op(tt(q, a, m["w"], ALU.mult))
                    op(tt(lb, la, q, ALU.add))
                    op(tt(a, a, m["bh"], ALU.mult))
                    op(tt(a, a, m["kq"], ALU.add))
                    op(tt(a, a, NEG1, ALU.pow))
                    op(tt(q, a, m["bb"], ALU.mult))
                    op(tt(a, q, m["it"], ALU.mult))
                    op(tt(tc, d, lb, ALU.subtract))
                    op(tt(a, a, tc, ALU.mult))
                    op(tt(tc, tb, a, ALU.add))
                    clip(tc, tc, m["tlo"], m["thi"])

                before_count(t0, t1)
                pool.wait_ge(act_step, base + 3)
                secant(t1, t2, m["l0"], m["l1"], m["g0"], m["g1"])
                ts(m["nt"], t2, -1.0, None, ALU.mult).then_inc(pool_t, 1)
                op(ts(q, q, KQ, None, ALU.mult))
                before_count(t1, t2)
                pool.wait_ge(act_step, base + 4)
                secant(t2, t0, m["l1"], m["l0"], m["g1"], m["g2"])
                op(ts(a, q, SHIFT, None, ALU.mult))
                op(tt(a, a, t0, ALU.add))
                op(ts(b, m["g2"], 40.0 - N, 2.0, ALU.is_le, ALU.mult))
                ts(q, q, KQ, None, ALU.mult)
                for v in range(2):
                    last = ts(m["hi"][:, v:v + 1], a[:, v:v + 1], b[:, v:v + 1], None, ALU.max)
                last.then_inc(pool_t, 1)

            rstd(0)
            for s in range(STEPS):
                def group(g):
                    for u in range(2):
                        pair(s, 2 * g + u, u)
                with pool.Fori(0, GROUPS) as g:
                    group(g)
            rstd(1)
            rstd(2)

        @block.scalar
        def _(act):
            a_ = nc.scalar.activation

            def squares(n, dst, src):
                act.wait_ge(ln_a, n + 1)
                a_(dst, src, ACT.Square).then_inc(ln_b, 1)

            def setup(s):
                chunks = N // 512

                def features(c):
                    i = chunks * s + c
                    act.wait_ge(su_xt, i + 1)
                    if c >= 2:
                        act.wait_ge(su_qk, i - 1)
                    a_(pt[c % 2][:], aux[c % 2][:], ACT.Copy).then_inc(su_xts, 1)

                features(0)
                for c in range(chunks):
                    if c + 1 < chunks:
                        features(c + 1)
                    act.wait_ge(su_q1, chunks * s + c + 1)
                    a_(q1s, sacc[0:64, :], ACT.Copy).then_inc(su_q1s, 1)

            def exp(s, pr, k, v):
                gp = s * PAIRS + pr
                m = stat[k]
                if v == 0:
                    act.wait_ge(neg_ready, gp + 1)
                last = a_(e[k][v][:], e[k][v][:], ACT.Exp, bias=m["negm"][:, v:v + 1], scale=LS,
                          accum_out=m["z"][:, v:v + 1])
                if v == 1:
                    last.then_inc(act_step, 1)

            def probe(s, pr, k, n, name, v, first=False, last=False):
                act.drain()
                if first:
                    act.wait_ge(pool_t, thresholds_before(s, pr) + n + 1)
                m = stat[k]
                i = a_(junk[:], e[k][v][:], ACT.Relu if name == "f" else ACT.Sign,
                       bias=m["nt"][:, v:v + 1], accum_out=m[name][:, v:v + 1])
                if last:
                    i.then_inc(act_step, 1)

            def transposed(s, pr, lo, hi):
                gp = s * PAIRS + pr
                for i in range(lo, hi):
                    idx = 16 * gp + i
                    act.wait_ge(aux_ready, idx + 1)
                    if s > 0 or i >= 2 or not isinstance(pr, int) or pr > 0:
                        act.wait_ge(pt_used, idx - 1)
                    a_(pt[i % 2][:], aux[i % 2][:], ACT.Copy).then_inc(pt_ready, 1)

            EARLY = 4

            def phase(s, p, k, before, after):
                stops = (6, 12, 14)

                def late(lo, hi):
                    if before:
                        transposed(s, p - 2, lo, hi)
                exp(s, p, k, 0)
                late(EARLY, stops[0])
                exp(s, p, k, 1)
                late(stops[0], stops[1])
                probe(s, p, k, 0, "f", 0, first=True)
                late(stops[1], stops[2])
                probe(s, p, k, 0, "f", 1)
                late(stops[2], 16)
                probe(s, p, k, 0, "g0", 0)
                probe(s, p, k, 0, "g0", 1, last=True)
                probe(s, p, k, 1, "g1", 0, first=True)
                probe(s, p, k, 1, "g1", 1, last=True)
                probe(s, p, k, 2, "g2", 0, first=True)
                if after:
                    transposed(s, p - 1, 0, EARLY // 2)
                probe(s, p, k, 2, "g2", 1, last=True)
                if after:
                    transposed(s, p - 1, EARLY // 2, EARLY)

            squares(0, pm[0][:], e[0][0][:])
            for s in range(STEPS):
                setup(s)
                phase(s, 0, 0, False, False)
                phase(s, 1, 1, False, True)
                with act.Fori(1, GROUPS) as g:
                    phase(s, 2 * g, 0, True, True)
                    phase(s, 2 * g + 1, 1, True, True)
                transposed(s, PAIRS - 2, EARLY, 16)
                transposed(s, PAIRS - 1, 0, 16)
            squares(1, sq[:], h2[:])
            for g in range(GROUPS):
                for a in range(4):
                    i = 4 * g + a
                    act.wait_ge(fin_tr, i + 1)
                    if g > 0 and a == 0:
                        act.wait_ge(fin_z, g)
                    a_(FT[a], aux[a % 2][:], ACT.Copy).then_inc(fin_ts, 1)
            squares(2, sq[:], h2[:])

        @block.vector
        def _(dve):
            v_ = nc.vector
            B = "p t d -> p t d"

            def op(ins):
                dve.drain()

            def ln_centre(n, buf, w_out=None):
                b3 = by_tile(buf)
                mean = st32[:, 0:T]
                op(v_.tensor_reduce(mean, b3, AX.X, ALU.add))
                op(v_.tensor_scalar(mean, mean, 1.0 / D, None, ALU.mult))
                v_.tensor_tensor(b3, b3, mean.unsqueeze(2).broadcast_to([P, T, D]), ALU.subtract).then_inc(ln_a, 1)

            def ln_var(n, sqb):
                dve.wait_ge(ln_b, n + 1)
                v_.tensor_reduce(st32[:, 2 * T:3 * T], by_tile(sqb), AX.X, ALU.add).then_inc(ln_c, 1)
                dve.wait_ge(ln_d, n + 1)

            rstd_b = st32[:, 2 * T:3 * T].unsqueeze(2).broadcast_to([P, T, D])

            def relu_rows(dst3, src):
                v_.scalar_tensor_tensor(dst3, by_tile(src), 0.0, rstd_b, ALU.max, ALU.mult).then_inc(h_ready, 1)

            def split(s):
                for c in range(N // 512):
                    i = 8 * s + c
                    cols = slice(512 * c, 512 * (c + 1))
                    dve.wait_ge(su_qk, i + 1)
                    qp, kp = lg[c % 2][:, 0:512], lg[c % 2][:, 512:1024]
                    v_.tensor_scalar(qhi, qp, QS, None, ALU.mult)
                    op(v_.tensor_scalar(k_hi[:, cols], kp, QS, None, ALU.mult))
                    v_.tensor_copy(q16[0:64, cols], qhi[0:64, :])
                    v_.scalar_tensor_tensor(q16[64:128, cols], qp[64:128, :], QS, qhi[64:128, :], ALU.mult, ALU.subtract)
                    v_.scalar_tensor_tensor(k_lo[:, cols], kp, QS, k_hi[:, cols], ALU.mult, ALU.subtract
                                            ).then_inc(su_split, 1)
                    dve.drain()
                op(v_.tensor_reduce(ks[:], k_hi[:], AX.X, ALU.add))
                v_.tensor_scalar(ks16[:], ks[:], 1.0 / N, None, ALU.mult).then_inc(su_ks, 1)
                dve.wait_ge(su_mu, s + 1)
                v_.tensor_scalar(mu_row[:], sacc[:, 0:T], LS, None, ALU.mult).then_inc(su_done, 1)
                dve.drain()

            def evacuate(s, pr, k):
                gp = s * PAIRS + pr
                for v in range(2):
                    for c in range(NCH):
                        i = v * NCH + c
                        dve.wait_ge(l_ready, 2 * NCH * gp + i + 1)
                        v_.tensor_scalar(e[k][v][:, CH * c:CH * (c + 1)], lg[i % 2][:], 1.0, None, ALU.mult, ALU.max,
                                         accum_out=mx[:, i:i + 1]).then_inc(l_evac, 1)
                dve.drain()
                m = stat[k]
                op(v_.tensor_reduce(sm[:, 60:62], mx[:].rearrange("p (v c) -> p v c", c=NCH), AX.X, ALU.max))
                op(v_.tensor_scalar(m["negm"][:], sm[:, 60:62], -LS, None, ALU.mult))
                v_.tensor_tensor(m["mu"][:], mu_row[:, bass.ds(2 * pr, 2)], m["negm"][:], ALU.add).then_inc(neg_ready, 1)
                dve.drain()

            c3 = cand[:].rearrange("p (v s m) -> p v s m", v=2, m=8)
            LH, V8, TC, OK, DONE, TS, LOB, HIB, HI, A1, A2, A3, PAR = (sm[:, 2 * i:2 * i + 2] for i in range(13))

            def window(k):
                for v in range(2):
                    for c in range(NWC):
                        w, cols = win[c % 2], slice(WC * c, WC * (c + 1))
                        op(v_.scalar_tensor_tensor(w[:], e[k][v][:, cols], HI[:, v:v + 1], e[k][v][:, cols], ALU.is_lt,
                                                   ALU.mult, accum_out=lh[:, NWC * v + c:NWC * v + c + 1]))
                        for sg in range(WC // SEG):
                            v_.max(c3[:, v, WC // SEG * c + sg, :], w[:, SEG * sg:SEG * (sg + 1)])
                v_.tensor_reduce(LH, lh[:].rearrange("p (v c) -> p v c", v=2), AX.X, ALU.add)
                dve.drain()

            def window_search(k):
                d = stat[k]["d"]
                v_.tensor_reduce(V8, c3[:, :, :, 7], AX.X, ALU.max)
                for r in range(ROUNDS):
                    for v in range(2):
                        v_.max(top[:, NTOP * v + 8 * r:NTOP * v + 8 * (r + 1)], cand[:, NSEG * 8 * v:NSEG * 8 * (v + 1)])
                    dve.drain()
                    if r < ROUNDS - 1:
                        for v in range(2):
                            cv = cand[:, NSEG * 8 * v:NSEG * 8 * (v + 1)]
                            v_.match_replace(cv, top[:, NTOP * v + 8 * r:NTOP * v + 8 * (r + 1)], cv, -1.0)
                        dve.drain()
                for v in range(2):
                    c = slice(NTOP * v, NTOP * (v + 1))
                    v_.tensor_tensor_scan(pre[:, c], ones[:], top[:, c], LH[:, v:v + 1], ALU.mult, ALU.subtract)
                dve.drain()
                for v in range(2):
                    c = slice(NTOP * v, NTOP * (v + 1))
                    v_.scalar_tensor_tensor(wn[:, c], pre[:, c], d[:, v:v + 1], top[:, c], ALU.is_le, ALU.mult)
                v_.tensor_tensor(A1, LH, d[:], ALU.is_gt)
                dve.drain()
                op(v_.tensor_reduce(TC, wn[:].rearrange("p (v c) -> p v c", v=2), AX.X, ALU.max))
                op(v_.tensor_tensor(A2, TC, V8, ALU.is_gt))
                op(v_.tensor_tensor(OK, A1, A2, ALU.mult))

            def open_rows(reg, OK_ALL):
                op(v_.tensor_tensor(flag[:, 0:1], OK_ALL[:, 0:1], OK_ALL[:, 1:2], ALU.mult))
                op(v_.transpose(flag_t[:], flag[:]))
                op(v_.tensor_reduce(flag_t[:, 0:1], flag_t[:, 0:32], AX.X, ALU.min))
                for q in range(1, 4):
                    v_.tensor_copy(flag_t[0:1, q:q + 1], flag_t[32 * q:32 * q + 1, 0:1])
                dve.drain()
                op(v_.tensor_reduce(flag_i[0:1, 0:1], flag_t[0:1, 0:4], AX.X, ALU.min))
                dve.load(reg, flag_i[0:1, 0:1])

            def retry(k, reg):
                m = stat[k]
                d, q = m["d"][:], m["q"][:]
                op(v_.tensor_tensor(A1, LH, d, ALU.is_gt))
                op(v_.tensor_scalar(A2, A1, -4.0, 4.0, ALU.mult, ALU.add))
                op(v_.tensor_tensor(A2, A2, HI, ALU.add))
                op(v_.tensor_tensor(HIB, HIB, A2, ALU.min))
                op(v_.tensor_scalar(A1, A1, -1.0, 1.0, ALU.mult, ALU.add))
                op(v_.tensor_tensor(A1, A1, HI, ALU.mult))
                op(v_.tensor_tensor(LOB, LOB, A1, ALU.max))
                op(v_.reciprocal(A1, HI))
                op(v_.tensor_tensor(A2, d, LH, ALU.subtract))
                op(v_.tensor_tensor(A1, A1, A2, ALU.mult))
                op(v_.tensor_scalar(A1, A1, 1.0 / KQ, SHIFT / KQ, ALU.mult, ALU.add))
                op(v_.tensor_tensor(A1, A1, q, ALU.mult))
                op(v_.tensor_tensor(A1, A1, HI, ALU.add))
                op(v_.tensor_tensor(A2, LOB, HIB, ALU.add))
                op(v_.tensor_scalar(A2, A2, 0.5, None, ALU.mult))
                op(v_.tensor_scalar(PAR, PAR, -1.0, 1.0, ALU.mult, ALU.add))
                op(v_.tensor_tensor(A3, A1, LOB, ALU.is_gt))
                op(v_.tensor_tensor(A3, A3, PAR, ALU.mult))
                op(v_.tensor_tensor(OK, A1, HIB, ALU.is_lt))
                op(v_.tensor_tensor(A3, A3, OK, ALU.mult))
                op(v_.tensor_tensor(A1, A1, A2, ALU.subtract))
                op(v_.tensor_tensor(A1, A1, A3, ALU.mult))
                op(v_.tensor_tensor(HI, A1, A2, ALU.add))
                window(k)
                window_search(k)
                settle()
                op(v_.scalar_tensor_tensor(A1, LOB, EPS_COLLAPSE, HIB, ALU.mult, ALU.is_ge))
                op(v_.tensor_scalar(A2, DONE, -1.0, 1.0, ALU.mult, ALU.add))
                op(v_.tensor_tensor(A1, A1, A2, ALU.mult))
                op(v_.tensor_tensor(A2, A1, LOB, ALU.mult))
                op(v_.tensor_tensor(TS, TS, A2, ALU.add))
                op(v_.tensor_tensor(DONE, DONE, A1, ALU.add))
                open_rows(reg, DONE)

            def settle():
                op(v_.tensor_scalar(A1, DONE, -1.0, 1.0, ALU.mult, ALU.add))
                op(v_.tensor_tensor(A1, A1, OK, ALU.mult))
                op(v_.tensor_tensor(A2, A1, TC, ALU.mult))
                op(v_.tensor_tensor(TS, TS, A2, ALU.add))
                op(v_.tensor_tensor(DONE, DONE, A1, ALU.add))

            def attended(s, pr, u):
                gp = s * PAIRS + pr
                dve.wait_ge(pt_used, 16 * gp + 16)
                dst = xaE if s == 0 else hE
                for v in range(2):
                    v_.reciprocal(sm[:, 40 + v:41 + v], pv[:, DE * v + D:DE * v + D + 1])
                if u == 0:
                    v_.tensor_copy(half[:, 0:D + 1 if s == 0 else D], pv[:, RS:RS + (D + 1 if s == 0 else D)])
                dve.drain()
                for v in range(2):
                    last = v_.tensor_scalar(row_tile(dst, 2 * pr + v), pv[:, DE * v:DE * v + D], sm[:, 40 + v:41 + v],
                                            None, ALU.mult)
                last.then_inc(pv_read, 1)
                dve.drain()

            def scaled(s, g):
                dve.wait_ge(s_used[1], (s * GROUPS + g + 1) * NSC)
                w = fw[s]
                prev = src_f[s][:, bass.ds(g * (4 * w), 4 * w)].rearrange("p (t d) -> p t d", d=w)[:, :, 0:D]
                dst = xf[:, bass.ds(g * (4 * D), 4 * D)] if s == 0 else zf[:]
                z3 = sacc[:, 0:3 * DE].rearrange("p (t d) -> p t d", d=DE)
                t3 = by_tile(zf[:], 4)
                if s == 0:
                    v_.tensor_scalar(rs[:, 0:3], z3[:, :, D], 1.0, None, ALU.add)
                    v_.scalar_tensor_tensor(rs[:, 3:4], pv[:, RS + D:RS + D + 1], 1.0, half[:, D:D + 1], ALU.add, ALU.add)
                else:
                    if not isinstance(g, int) or g > 0:
                        dve.wait_ge(zf_stored, 16 * g)
                v_.tensor_tensor(t3[:, 0:3, :], z3[:, :, 0:D], prev[:, 0:3, :], ALU.add)
                op(v_.tensor_tensor(t3[:, 3, :], prop(3), prev[:, 3, :], ALU.add))
                v_.tensor_tensor(t3[:, 3, :], t3[:, 3, :], half[:, 0:D], ALU.add)
                dve.drain()
                if s == 0:
                    op(v_.reciprocal(rinv[:, bass.ds(g * 4, 4)], rs[:, 0:4]))
                v_.tensor_tensor(by_tile(dst, 4), t3, rinv[:, bass.ds(g * 4, 4)].unsqueeze(2).broadcast_to([P, 4, D]),
                                 ALU.mult).then_inc(s_scaled, 1)
                dve.drain()

            def finish(s, pr, k, reg, between):
                gp = s * PAIRS + pr
                m = stat[k]
                dve.wait_ge(pool_t, thresholds_before(s, pr + 1))
                v_.tensor_copy(HI, m["hi"][:])
                v_.memset(PAR, 0.0)
                v_.tensor_scalar(LOB, m["d"][:], 0.5 / N, None, ALU.mult)
                v_.memset(HIB, 2.5)
                dve.drain()
                window(k)
                between()
                window_search(k)
                v_.tensor_copy(DONE, OK)
                v_.tensor_tensor(TS, OK, TC, ALU.mult)
                open_rows(reg, OK)
                with dve.While(lambda: dve.snap(reg) < 1):
                    retry(k, reg)
                if s > 0 or not isinstance(pr, int) or pr > 0:
                    dve.wait_ge(aux_ready, 16 * gp)
                for v in range(2):
                    v_.scalar_tensor_tensor(pm[v][:], e[k][v][:], TS[:, v:v + 1], e[k][v][:], ALU.is_ge, ALU.mult
                                            ).then_inc(masked, 1)
                dve.drain()

            reg = dve.alloc_register("open_rows")
            v_.memset(flag[:], 0.0)
            v_.memset(ones[:], 1.0)
            for buf in (hE, xaE):
                last = v_.memset(by_tile(buf[:], T, DE)[:, :, D:DE], 1.0)
            last.then_inc(consts, 1)
            dve.wait_ge(ld_x, 16)
            ln_centre(0, e[0][0][:])
            ln_var(0, pm[0][:])
            relu_rows(by_tile(hE[:], T, DE)[:, :, 0:D], e[0][0][:])
            dve.drain()
            for s in range(STEPS):
                split(s)
                evacuate(s, 0, 0)
                evacuate(s, 1, 1)

                def group(g, first=False, last=False):
                    for u in range(2):
                        pr = 2 * g + u

                        def between():
                            if not (first and u == 0):
                                attended(s, pr - 1, 1 - u)
                            if u == 0 and not first:
                                scaled(s, g - 1)
                        finish(s, pr, u, reg, between)
                        if not last:
                            evacuate(s, pr + 2, u)
                group(0, first=True)
                with dve.Fori(1, GROUPS - 1) as g:
                    group(g)
                group(GROUPS - 1, last=True)
                attended(s, PAIRS - 1, 1)
                scaled(s, GROUPS - 1)
            v_.memset(sm[:, 42:43], 0.0).then_inc(fin_h, 1)
            dve.wait_ge(ld_f, 16 * 8)
            v_.tensor_copy(h2[:], x_fin[:])
            dve.drain()
            ln_centre(1, h2[:])
            dve.wait_ge(ln_b, 2)
            v_.tensor_reduce(st32[:, 2 * T:3 * T], by_tile(sq[:]), AX.X, ALU.add).then_inc(ln_c, 1)
            dve.wait_ge(ln_d, 2)
            op(v_.scalar_tensor_tensor(by_tile(h2[:]), by_tile(h2[:]), 0.0, rstd_b, ALU.max, ALU.mult))
            for g in range(GROUPS):
                dve.wait_ge(fin_z, g + 1)
                c = slice(512 * g, 512 * (g + 1))
                v_.tensor_tensor(h2[:, c], h2[:, c], lg[g % 2][:, 0:512], ALU.add).then_inc(fin_free, 1)
            dve.drain()
            ln_centre(2, h2[:])
            dve.wait_ge(ln_b, 3)
            v_.tensor_reduce(st32[:, 2 * T:3 * T], by_tile(sq[:]), AX.X, ALU.add).then_inc(ln_c, 1)
            dve.wait_ge(ln_d, 3)
            op(v_.tensor_tensor(by_tile(h2[:]), by_tile(h2[:]), rstd_b, ALU.mult))
            op(v_.tensor_tensor(by_tile(h2[:]), by_tile(h2[:]), gsb.unsqueeze(1).broadcast_to([P, T, D]), ALU.mult))
            op(v_.tensor_tensor(by_tile(h2[:]), by_tile(h2[:]), bsb.unsqueeze(1).broadcast_to([P, T, D]), ALU.add))
            v_.tensor_tensor(h2[:], h2[:], x_fin[:], ALU.add).then_inc(fin_out, 1)

        @block.tensor
        def _(pe):
            mm, tr = nc.tensor.matmul, nc.tensor.transpose

            def setup(s):
                if s == 0:
                    pe.wait_ge(ld_w, 64)
                    pe.wait_ge(consts, 1)
                    pe.wait_ge(h_ready, 1)
                else:
                    pe.wait_ge(pv_read, PAIRS)
                    pe.wait_ge(s_scaled, GROUPS)
                chunks = N // 512

                def transposes(c):
                    i = chunks * s + c
                    if c >= 2:
                        pe.wait_ge(su_xts, i - 1)
                    for m in range(4):
                        last = tr(aux[c % 2][:, P * m:P * (m + 1)], row_tile(srcE[s], 4 * c + m), ident[:])
                    last.then_inc(su_xt, 1)

                transposes(0)
                transposes(1)
                for c in range(chunks):
                    i = chunks * s + c
                    pe.wait_ge(su_xts, i + 1)
                    if i > 0:
                        pe.wait_ge(su_q1s, i)
                    mm(sacc[0:64, :], w1[:], pt[c % 2][:], start=True, stop=True).then_inc(su_q1, 1)
                    if c >= 2:
                        pe.wait_ge(su_split, i - 1)
                    mm(lg[c % 2][:, 512:1024], w3[:], pt[c % 2][:], start=True, stop=True)
                    if c + 2 < chunks:
                        transposes(c + 2)
                    pe.wait_ge(su_q1s, i + 1)
                    mm(lg[c % 2][:, 0:512], w2[:], q1s, start=True, stop=True).then_inc(su_qk, 1)
                pe.wait_ge(su_ks, s + 1)
                for t in range(T):
                    last = mm(sacc[:, t:t + 1], q16[:, P * t:P * (t + 1)], ks16[:], start=True, stop=True)
                last.then_inc(su_mu, 1)
                pe.wait_ge(su_done, s + 1)

            def logits(s, pr, i):
                v, c = divmod(i, NCH)
                idx = 2 * NCH * (s * PAIRS + pr) + i
                if s > 0 or i >= 2 or not isinstance(pr, int) or pr > 0:
                    pe.wait_ge(l_evac, idx - 1)
                q = q16[:, bass.ds((2 * pr + v) * P, P)]
                for h in range(2):
                    o = lg[i % 2][:, 512 * h:512 * (h + 1)]
                    cols = slice(CH * c + 512 * h, CH * c + 512 * (h + 1))
                    mm(o, q, k_hi[:, cols], start=True, stop=False)
                    last = mm(o, q, k_lo[:, cols], start=False, stop=True)
                last.then_inc(l_ready, 1)

            def propagate(s, g, u):
                if u == 0 and (not isinstance(g, int) or g > 0):
                    pe.wait_ge(s_scaled, s * GROUPS + g)
                w = D + 1 if s == 0 else D
                for c in range(NSC):
                    cc = NSC * u + c
                    i = cc % 2
                    pe.wait_ge(s_loaded[i], 16 * ((s * GROUPS + g) * NSC + cc // 2 + 1))
                    for j in range(SJ):
                        n = cc * SJ + j
                        for m in range(4):
                            last = mm(prop(m, w), s_ring[i][:, 512 * j + P * m:512 * j + P * (m + 1)],
                                      src_f[s][:, n * fw[s]:n * fw[s] + w],
                                      start=n == 0 and m == 0 or c == j == 0 and m == 3,
                                      stop=n == T - 1 or m == 3 and c == NSC - 1 and j == SJ - 1,
                                      skip_group_check=True)
                    last.then_inc(s_used[i], 1)

            def attend(s, pr, v, q):
                idx = 16 * (s * PAIRS + pr) + 8 * v + q
                pe.wait_ge(pt_ready, idx + 1)
                for j in range(4):
                    t = 4 * q + j
                    last = mm(pv[:, DE * v:DE * v + D + 1], pt[q % 2][:, P * j:P * (j + 1)],
                              row_tile(srcE[s], t, D + 1), start=t == 0, stop=t == T - 1)
                last.then_inc(pt_used, 1)

            def iteration(s, g, u, last_group=False):
                pr = 2 * g + u
                gp = s * PAIRS + pr
                started = s > 0 or u > 0 or not isinstance(g, int) or g > 0
                if not last_group:
                    logits(s, pr + 2, 0)
                    logits(s, pr + 2, 1)
                if started:
                    pe.wait_ge(pv_read, gp)
                propagate(s, g, u)
                for n in range(16):
                    v, q = divmod(n, 8)
                    if q == 0:
                        pe.wait_ge(masked, 2 * gp + v + 1)
                    if started or n >= 2:
                        pe.wait_ge(pt_ready, 16 * gp + n - 1)
                    for m in range(4):
                        t = 4 * q + m
                        last = tr(aux[q % 2][:, P * m:P * (m + 1)], pm[v][:, P * t:P * (t + 1)], ident[:])
                    last.then_inc(aux_ready, 1)
                    if n in (1, 2, 3) and not last_group:
                        logits(s, pr + 2, 2 * n)
                        logits(s, pr + 2, 2 * n + 1)
                    if n > 0:
                        attend(s, pr, *divmod(n - 1, 8))
                attend(s, pr, 1, 7)

            for s in range(STEPS):
                setup(s)
                for pr in range(2):
                    for i in range(2 * NCH):
                        logits(s, pr, i)
                for u in range(2):
                    iteration(s, 0, u)
                with pe.Fori(1, GROUPS - 1) as g:
                    for u in range(2):
                        iteration(s, g, u)
                for u in range(2):
                    iteration(s, GROUPS - 1, u, last_group=True)
            pe.wait_ge(ld_f, 16 * 8)
            rows = ((xf, D), (xaE, DE), (fin_src, D), (hE, DE))
            for g in range(GROUPS):
                for a, (src, w) in enumerate(rows):
                    i = 4 * g + a
                    if i >= 2:
                        pe.wait_ge(fin_ts, i - 1)
                    for m in range(4):
                        t = 4 * g + m
                        last = tr(aux[a % 2][:, P * m:P * (m + 1)], src[:, w * t:w * t + D], ident[:])
                    last.then_inc(fin_tr, 1)
                pe.wait_ge(fin_ts, 4 * g + 4)
                if g >= 2:
                    pe.wait_ge(fin_free, g - 1)
                for m in range(4):
                    for a in range(4):
                        last = mm(lg[g % 2][:, P * m:P * (m + 1)], FT[a][:, P * m:P * (m + 1)], us[a],
                                  start=a == 0, stop=a == 3)
                last.then_inc(fin_z, 1)

    return nc


_IN = ["x", "adj_t", "w1_t", "w2_tt", "w3_tt", "u_t", "gain", "shift", "ident"]


def kernel(x, adj, L0_gnn_W1, L0_gnn_W2, L0_gnn_W3, L0_gnn_U1, L0_gnn_U2, L0_gnn_ln_g, L0_gnn_ln_b):
    import numpy as np
    import concourse.bacc as bacc
    from concourse import mybir
    from concourse.bass_utils import run_bass_kernel_spmd

    c = np.ascontiguousarray
    x, adj, w1, w2, w3, u1, u2 = (np.asarray(a) for a in (x, adj, L0_gnn_W1, L0_gnn_W2, L0_gnn_W3, L0_gnn_U1, L0_gnn_U2))
    n = x.shape[0]
    adj_t = c(adj.reshape(n // 512, 512, n // 256, 2, 128).transpose(0, 2, 4, 3, 1)).reshape(n // 512, n // 256, 128, 1024)
    arrays = {
        "x": c(x), "adj_t": adj_t, "w1_t": c(w1.T),
        "w2_tt": c(np.concatenate([w2.T, w2.T], 1)), "w3_tt": c(np.concatenate([w3.T, w3.T], 1)),
        "u_t": c(np.stack([u1[0].T, u2[0].T, u1[1].T, u2[1].T])),
        "gain": c(np.broadcast_to(np.asarray(L0_gnn_ln_g), (128, x.shape[1]))),
        "shift": c(np.broadcast_to(np.asarray(L0_gnn_ln_b), (128, x.shape[1]))),
        "ident": np.eye(128, dtype=np.float32),
    }
    nc = bacc.Bacc("TRN2", target_bir_lowering=False, num_devices=1)
    args = [nc.dram_tensor(f"in_{k}", arrays[k].shape, mybir.dt.from_np(arrays[k].dtype), kind="ExternalInput").ap()
            for k in _IN]
    out = nc.dram_tensor("out_0", x.shape, mybir.dt.float32, kind="ExternalOutput").ap()
    rows = nc.dram_tensor("xf_rows", (n // 512, 128, 512), mybir.dt.float32, kind="Internal").ap()
    top_p_graph_mix(nc, *args, out, rows)
    r = run_bass_kernel_spmd(nc, [{f"in_{k}": arrays[k] for k in _IN}], core_ids=[0])
    return r.results[0]["out_0"]
```

```python
import concourse.bass as bass
from concourse import mybir
from contextlib import ExitStack


def top_p_graph_mix(nc, x, adj_t, w1_t, w2_tt, w3_tt, u_t, gain, shift, ident_d, out, xf_rows):
    f32, f16, bf16, i32 = mybir.dt.float32, mybir.dt.float16, mybir.dt.bfloat16, mybir.dt.int32
    ALU, ACT, AX = mybir.AluOpType, mybir.ActivationFunctionType, mybir.AxisListType

    P = 128
    N, D = x.shape
    T = N // P
    PAIRS = T // 2
    GROUPS = T // 4
    STEPS = 2
    DE = D + 2
    CH = 1024
    NCH = N // CH
    SJ = 2
    NSC = T // 2 // SJ
    SEG = 256
    NSEG = N // SEG
    WC = 1024
    NWC = N // WC
    ROUNDS = 6
    NTOP = 8 * ROUNDS
    KQ = 10.0
    SHIFT = 13.0
    QS = 256.0
    LS = 1.0 / (QS * QS)
    TAIL = 0.1
    Z10 = 1.2815516
    B10 = 1.7549833
    LN_EPS = 1e-5
    LNR = 2.0 ** -8
    EPS_COLLAPSE = 1.0 + 2.0 ** -22

    with ExitStack() as ctx:
        def sb(name, shape, dt=f32):
            return ctx.enter_context(nc.sbuf_tensor(name, shape, dt))

        def sem(name):
            return ctx.enter_context(nc.semaphore(name))

        e = [[sb(f"e{k}{v}", [P, N]) for v in range(2)] for k in range(2)]
        pm = [sb(f"pm{v}", [P, N]) for v in range(2)]
        hE = sb("hE", [P, T * DE])
        xaE = sb("xaE", [P, T * DE])
        xf = sb("xf", [P, T * D])
        q16 = sb("q16", [P, N], f16)
        k_hi = sb("k_hi", [P, N], f16)
        k_lo = sb("k_lo", [P, N], f16)
        junk = sb("junk", [P, N], bf16)
        win = [sb(f"win{i}", [P, WC]) for i in range(2)]
        s_ring = [sb(f"s_ring{i}", [P, SJ * 512]) for i in range(2)]
        pt = [sb(f"pt{i}", [P, 512]) for i in range(2)]
        q1s_b = sb("q1s", [P, 512])
        q1s = q1s_b[0:64, :]
        half = q1s_b[:, 0:D + 1]
        ident = sb("ident", [P, P])
        ones = sb("ones", [P, NTOP])
        w1 = sb("w1", [P, 64])
        w2 = sb("w2", [64, P])
        w3 = sb("w3", [P, P])
        rx_group = sb("rx_group", [P, 512])
        qhi = rx_group[:].bitcast(f16)[:, 0:512]
        rinv = sb("rinv", [P, T])
        rs = sb("rs", [P, 8])
        mu_row = sb("mu_row", [P, T])
        ks = sb("ks", [P, 1])
        ks16 = sb("ks16", [P, 1], f16)
        st32 = sb("st32", [P, 4 * T])
        mx = sb("mx", [P, 2 * NCH])
        lh = sb("lh", [P, 2 * NWC])
        cand = sb("cand", [P, 2 * NSEG * 8])
        top = sb("top", [P, 2 * NTOP])
        pre = sb("pre", [P, 2 * NTOP])
        wn = sb("wn", [P, 2 * NTOP])
        sm = sb("sm", [P, 64])
        flag = sb("flag", [P, 32])
        flag_t = sb("flag_t", [P, 32])
        flag_i = sb("flag_i", [P, 2], i32)
        cst = sb("cst", [P, 16])
        STATS = ("negm", "mu", "z", "f", "g0", "g1", "g2", "hi", "q", "d",
                  "t0", "t1", "t2", "pw", "npw", "l0", "l1", "lo", "tlo", "thi", "th", "w", "bh", "kq", "bb", "it", "a", "b", "c")
        stats = [sb(f"stats{k}", [P, 2 * len(STATS)]) for k in range(2)]
        stat = [{n: stats[k][:, 2 * i:2 * i + 2] for i, n in enumerate(STATS)} for k in range(2)]

        lg = [ctx.enter_context(nc.psum_tensor(f"lg{i}", [P, CH], f32)) for i in range(2)]
        aux = [ctx.enter_context(nc.psum_tensor(f"aux{i}", [P, 512], f32)) for i in range(2)]
        sacc = ctx.enter_context(nc.psum_tensor("sacc", [P, 512], f32))
        pv = ctx.enter_context(nc.psum_tensor("pv", [P, 512], f32))
        RS = 264

        def sems(*names):
            return [sem(name) for name in names]

        x_loaded, weights_loaded, final_loaded = sems("x_loaded", "weights_loaded", "final_loaded")
        ones_ready, h_ready = sems("ones_ready", "h_ready")
        ln_centred, ln_squared, ln_variance, ln_rstd = sems("ln_centred", "ln_squared", "ln_variance", "ln_rstd")
        x_transposed, xt_copied, q1_ready, q1_copied = sems("x_transposed", "xt_copied", "q1_ready", "q1_copied")
        qk_ready, qk_split, mean_key, mean_logits, mean_read = sems("qk_ready", "qk_split", "mean_key",
                                                                    "mean_logits", "mean_read")
        adj_loaded = [sem(f"adj_loaded{i}") for i in range(2)]
        adj_used = [sem(f"adj_used{i}") for i in range(2)]
        logits_ready, logits_read, max_ready = sems("logits_ready", "logits_read", "max_ready")
        sums_ready, threshold_ready = sems("sums_ready", "threshold_ready")
        masked = sem("masked")
        tiles_transposed, tiles_copied, tiles_used = sems("tiles_transposed", "tiles_copied", "tiles_used")
        pv_read = sem("pv_read")
        rx_ready, rx_stored = sems("rx_ready", "rx_stored")
        fin_transposed, fin_copied, fin_product, fin_read = sems("fin_transposed", "fin_copied", "fin_product",
                                                                 "fin_read")
        fin_rows, out_stored = sems("fin_rows", "out_stored")

        def row_tile(buf, t, w=D):
            return buf[:, bass.ds(t * DE, w)]

        srcE = [hE, xaE]
        src_f = [hE, xf]
        fw = [DE, D]
        fin_src = e[0][1]
        x_fin = e[0][0]
        h2 = e[1][0]
        sq = e[1][1]
        FT = [pm[0][:, 512 * a:512 * (a + 1)] for a in range(4)]
        fin_w = k_hi[:].bitcast(f32)
        gsb, bsb = fin_w[:, 0:D], fin_w[:, D:2 * D]
        us = [fin_w[:, D * (2 + a):D * (3 + a)] for a in range(4)]
        FIN_LOADS = 7

        def prop(m, w=D):
            return sacc[:, DE * m:DE * m + w] if m < 3 else pv[:, RS:RS + w]

        def by_tile(buf, n=T, w=D):
            return buf.rearrange("p (t d) -> p t d", d=w)

        def thresholds_before(s, pr):
            return 4 * (s * PAIRS + pr)

        def sums_before(s, pr):
            return 5 * (s * PAIRS + pr)

        block = ctx.enter_context(nc.Block())

        @block.sync
        def _(sp):
            sp.dma_start(by_tile(e[0][0][:]), x.rearrange("(t p) d -> p t d", p=P)).then_inc(x_loaded, 16)
            for dst, src in ((w1, w1_t), (w2, w2_tt), (w3, w3_tt), (ident, ident_d)):
                sp.dma_start(dst[:], src).then_inc(weights_loaded, 16)
            for s in range(STEPS):
                def store(g):
                    sp.wait_ge(rx_ready, GROUPS + g + 1)
                    sp.dma_start(xf_rows[bass.ds(g, 1)].rearrange("g p n -> (g p) n"),
                                 rx_group[:]).then_inc(rx_stored, 16)

                def blocks(g, first=False):
                    for c in range(2 * NSC):
                        i = c % 2
                        if c == 2 and s == 1 and not (isinstance(g, int) and g == 0):
                            store(g - 1)
                        if not (first and c < 2):
                            sp.wait_ge(adj_used[i], (s * GROUPS + g) * NSC + c // 2)
                        sp.dma_start(s_ring[i][:], adj_t[bass.ds(g, 1), c].rearrange("g p n -> (g p) n")
                                     ).then_inc(adj_loaded[i], 16)
                blocks(0, s == 0)
                with sp.Fori(1, GROUPS) as g:
                    blocks(g)
            sp.wait_ge(masked, 2 * (2 * PAIRS - 1))
            sp.dma_start(by_tile(x_fin[:]), x.rearrange("(t p) d -> p t d", p=P)).then_inc(x_loaded, 16)
            sp.wait_ge(logits_ready, 2 * NCH * 2 * PAIRS)
            for a in range(4):
                sp.dma_start(us[a], u_t[a]).then_inc(final_loaded, 16)
            sp.dma_start(gsb, gain).then_inc(final_loaded, 16)
            sp.dma_start(bsb, shift).then_inc(final_loaded, 16)
            sp.wait_ge(rx_stored, 16 * (GROUPS - 1))
            sp.dma_start(fin_src[:, 0:(GROUPS - 1) * 4 * D].rearrange("p (g n) -> p g n", n=4 * D),
                         xf_rows[0:GROUPS - 1].rearrange("g p n -> p g n")).then_inc(final_loaded, 16)
            for g in range(GROUPS):
                sp.wait_ge(fin_rows, g + 1)
                sp.dma_start(out.rearrange("(t p) d -> p t d", p=P)[:, 4 * g:4 * (g + 1), :],
                             by_tile(h2[:, 512 * g:512 * (g + 1)], 4)).then_inc(out_stored, 16)
            sp.wait_ge(out_stored, 16 * GROUPS)

        @block.gpsimd
        def _(pool):
            def op(ins):
                pool.drain()

            g_ = nc.gpsimd
            tt, ts = g_.tensor_tensor, g_.tensor_scalar
            for c, val in enumerate((0.5, 2.718281828459045, -1.0, -0.5, 1.0 / N, LNR, -LNR)):
                g_.memset(cst[:, 2 * c:2 * c + 2], val)
            pool.drain()
            HALF, EULER, NEG1, NEGH, R_N, POSR, NEGR = (cst[:, 2 * c:2 * c + 2] for c in range(7))

            def rstd(n, cols=slice(2 * T, 3 * T)):
                pool.wait_ge(ln_variance, n + 1)
                v = st32[:, cols]
                op(ts(v, v, 1.0 / D, LN_EPS, ALU.mult, ALU.add))
                tt(v, v, NEGH[:, 0:1].broadcast_to([P, v.shape[1]]), ALU.pow).then_inc(ln_rstd, 1)

            def pair(s, pr, k):
                base = sums_before(s, pr)
                m = {n: t_[:] for n, t_ in stat[k].items()}
                z, d, t0, t1, t2, q, th, a, b, c = (m[n] for n in ("z", "d", "t0", "t1", "t2", "q", "th", "a", "b", "c"))

                def bounds(t, down, up):
                    for v in range(2):
                        c_ = slice(v, v + 1)
                        ts(m["tlo"][:, c_], t[:, c_], down, m["lo"][:, c_], ALU.mult, ALU.max)
                    op(ts(m["thi"], t, up, 0.98, ALU.mult, ALU.min))

                def clip(o, src, lo, hi, signal=False):
                    for v in range(2):
                        c_ = slice(v, v + 1)
                        last = ts(o[:, c_], src[:, c_], lo[:, c_], hi if isinstance(hi, float) else hi[:, c_],
                                  ALU.max, ALU.min)
                    if signal:
                        last.then_inc(threshold_ready, 1)
                    pool.drain()

                pool.wait_ge(sums_ready, base + 1)
                op(tt(a, z, R_N, ALU.mult))
                op(tt(b, a, NEGR, ALU.pow))
                op(tt(a, a, POSR, ALU.pow))
                op(tt(a, a, b, ALU.subtract))
                op(ts(b, m["mu"], 2.0 * LNR, None, ALU.mult))
                op(tt(a, a, b, ALU.subtract))
                op(ts(a, a, 1.0 / LNR, 1e-6, ALU.mult, ALU.max))
                op(tt(b, a, HALF, ALU.pow))
                op(tt(a, a, m["mu"], ALU.add))
                op(ts(c, b, -Z10, None, ALU.mult))
                op(tt(a, a, c, ALU.add))
                op(tt(t0, EULER, a, ALU.pow))
                op(ts(m["lo"], z, 1.01 * TAIL / N, None, ALU.mult))
                clip(t0, t0, m["lo"], 0.98, signal=True)
                bounds(t0, 0.25, 4.0)
                op(ts(d, z, TAIL, None, ALU.mult))
                op(tt(c, d, NEG1, ALU.pow))
                op(ts(m["pw"], b, 1.0 / B10, None, ALU.mult))
                op(ts(m["npw"], b, -1.0 / B10, None, ALU.mult))
                op(tt(q, t0, t0, ALU.mult))
                op(tt(q, q, m["pw"], ALU.mult))

                op(ts(th, t0, 0.5, None, ALU.mult))
                op(ts(a, t0, N / 2, None, ALU.mult))

                pool.wait_ge(sums_ready, base + 2)
                op(tt(a, a, m["f"], ALU.subtract))
                pool.wait_ge(sums_ready, base + 3)
                op(tt(b, m["g0"], th, ALU.mult))
                op(tt(m["l0"], a, b, ALU.add))
                op(tt(b, c, m["l0"], ALU.mult))
                op(ts(b, b, 1e-6, None, ALU.max))
                op(tt(c, b, m["npw"], ALU.pow))
                op(tt(t1, t0, c, ALU.mult))
                clip(t1, t1, m["tlo"], m["thi"], signal=True)
                op(ts(a, m["l0"], 1e-9, None, ALU.max))
                op(tt(a, a, NEG1, ALU.pow))
                op(tt(a, a, q, ALU.mult))
                op(ts(q, a, KQ, 2.0, ALU.mult, ALU.min))

                def before_count(ta, tb):
                    op(tt(m["w"], ta, tb, ALU.add))
                    op(ts(m["w"], m["w"], 0.25, None, ALU.mult))
                    op(tt(b, tb, ta, ALU.subtract))
                    op(ts(m["bh"], b, 0.5, None, ALU.mult))
                    op(ts(m["kq"], q, KQ, None, ALU.mult))
                    op(tt(b, b, b, ALU.mult))
                    op(tt(c, q, q, ALU.mult))
                    op(tt(m["bb"], b, c, ALU.add))
                    op(tt(m["it"], tb, NEG1, ALU.pow))
                    bounds(tb, 0.6, 1.6)

                def secant(tb, tc, la, lb, ga, gb, signal=False):
                    op(tt(a, gb, ga, ALU.subtract))
                    op(tt(q, a, m["w"], ALU.mult))
                    op(tt(lb, la, q, ALU.add))
                    op(tt(a, a, m["bh"], ALU.mult))
                    op(tt(a, a, m["kq"], ALU.add))
                    op(tt(a, a, NEG1, ALU.pow))
                    op(tt(q, a, m["bb"], ALU.mult))
                    op(tt(a, q, m["it"], ALU.mult))
                    op(tt(tc, d, lb, ALU.subtract))
                    op(tt(a, a, tc, ALU.mult))
                    op(tt(tc, tb, a, ALU.add))
                    clip(tc, tc, m["tlo"], m["thi"], signal)

                before_count(t0, t1)
                pool.wait_ge(sums_ready, base + 4)
                secant(t1, t2, m["l0"], m["l1"], m["g0"], m["g1"], signal=True)
                op(ts(q, q, KQ, None, ALU.mult))
                before_count(t1, t2)
                pool.wait_ge(sums_ready, base + 5)
                secant(t2, t0, m["l1"], m["l0"], m["g1"], m["g2"])
                op(ts(a, q, SHIFT, None, ALU.mult))
                op(tt(a, a, t0, ALU.add))
                op(ts(b, m["g2"], N - 40.0, 2.0, ALU.is_ge, ALU.mult))
                ts(q, q, KQ, None, ALU.mult)
                for v in range(2):
                    last = ts(m["hi"][:, v:v + 1], a[:, v:v + 1], b[:, v:v + 1], None, ALU.max)
                last.then_inc(threshold_ready, 1)

            rstd(0)
            for s in range(STEPS):
                def group(g):
                    for u in range(2):
                        pair(s, 2 * g + u, u)

                with pool.Fori(0, GROUPS) as g:
                    group(g)
            rstd(1)
            for g in range(GROUPS):
                rstd(2 + g, slice(2 * T + 4 * g, 2 * T + 4 * (g + 1)))

        @block.scalar
        def _(act):
            a_ = nc.scalar.activation

            def squares(n, dst, src):
                act.wait_ge(ln_centred, n + 1)
                a_(dst, src, ACT.Square).then_inc(ln_squared, 1)

            def setup(s):
                chunks = N // 512

                def features(c):
                    i = chunks * s + c
                    act.wait_ge(x_transposed, i + 1)
                    if c >= 2:
                        act.wait_ge(qk_ready, i - 1)
                    a_(pt[c % 2][:], aux[c % 2][:], ACT.Copy).then_inc(xt_copied, 1)

                features(0)
                for c in range(chunks):
                    if c + 1 < chunks:
                        features(c + 1)
                    act.wait_ge(q1_ready, chunks * s + c + 1)
                    a_(q1s, sacc[0:64, :], ACT.Copy).then_inc(q1_copied, 1)

            def exp(s, pr, k, v):
                gp = s * PAIRS + pr
                m = stat[k]
                if v == 0:
                    act.wait_ge(max_ready, gp + 1)
                last = a_(e[k][v][:], e[k][v][:], ACT.Exp, bias=m["negm"][:, v:v + 1], scale=LS,
                          accum_out=m["z"][:, v:v + 1])
                if v == 1:
                    last.then_inc(sums_ready, 1)

            def probe(s, pr, k, n, name, v, first=False, last=False):
                act.drain()
                if first:
                    act.wait_ge(threshold_ready, thresholds_before(s, pr) + n + 1)
                m = stat[k]
                i = a_(junk[:], e[k][v][:], ACT.Relu if name == "f" else ACT.Sign,
                       bias=m[f"t{n}"][:, v:v + 1], scale=-1.0, accum_out=m[name][:, v:v + 1])
                if last:
                    i.then_inc(sums_ready, 1)

            def transposed(s, pr, lo, hi):
                gp = s * PAIRS + pr
                for i in range(lo, hi):
                    idx = 16 * gp + i
                    act.wait_ge(tiles_transposed, idx + 1)
                    if s > 0 or i >= 2 or not isinstance(pr, int) or pr > 0:
                        act.wait_ge(tiles_used, idx - 1)
                    a_(pt[i % 2][:], aux[i % 2][:], ACT.Copy).then_inc(tiles_copied, 1)

            EARLY = 5

            def phase(s, p, k, before, after):
                stops = (7, 12, 14)

                def late(lo, hi):
                    if before:
                        transposed(s, p - 2, lo, hi)
                exp(s, p, k, 0)
                late(EARLY, stops[0])
                exp(s, p, k, 1)
                late(stops[0], stops[1])
                probe(s, p, k, 0, "f", 0, first=True)
                late(stops[1], stops[2])
                probe(s, p, k, 0, "f", 1, last=True)
                late(stops[2], 16)
                probe(s, p, k, 0, "g0", 0)
                probe(s, p, k, 0, "g0", 1, last=True)
                probe(s, p, k, 1, "g1", 0, first=True)
                probe(s, p, k, 1, "g1", 1, last=True)
                probe(s, p, k, 2, "g2", 0, first=True)
                if after:
                    transposed(s, p - 1, 0, EARLY // 2)
                probe(s, p, k, 2, "g2", 1, last=True)
                if after:
                    transposed(s, p - 1, EARLY // 2, EARLY)

            squares(0, pm[0][:], e[0][0][:])
            for s in range(STEPS):
                setup(s)
                phase(s, 0, 0, False, False)
                phase(s, 1, 1, False, True)
                with act.Fori(1, GROUPS) as g:
                    phase(s, 2 * g, 0, True, True)
                    phase(s, 2 * g + 1, 1, True, True)
                transposed(s, PAIRS - 2, EARLY, 16)
                transposed(s, PAIRS - 1, 0, 16)
            for g in range(GROUPS):
                for a in range(4):
                    i = 4 * g + a
                    act.wait_ge(fin_transposed, i + 1)
                    if g > 0 and a == 0:
                        act.wait_ge(fin_product, g)
                    a_(FT[a], aux[a % 2][:], ACT.Copy).then_inc(fin_copied, 1)

        @block.vector
        def _(dve):
            v_ = nc.vector

            def op(ins):
                dve.drain()

            def ln_centre(n, buf):
                b3 = by_tile(buf)
                mean = st32[:, 0:T]
                op(v_.tensor_reduce(mean, b3, AX.X, ALU.add))
                op(v_.tensor_scalar(mean, mean, 1.0 / D, None, ALU.mult))
                v_.tensor_tensor(b3, b3, mean.unsqueeze(2).broadcast_to([P, T, D]), ALU.subtract).then_inc(ln_centred, 1)

            def ln_var(n, sqb):
                dve.wait_ge(ln_squared, n + 1)
                v_.tensor_reduce(st32[:, 2 * T:3 * T], by_tile(sqb), AX.X, ALU.add).then_inc(ln_variance, 1)
                dve.wait_ge(ln_rstd, n + 1)

            rstd_b = st32[:, 2 * T:3 * T].unsqueeze(2).broadcast_to([P, T, D])

            def relu_rows(dst3, src):
                v_.scalar_tensor_tensor(dst3, by_tile(src), 0.0, rstd_b, ALU.max, ALU.mult).then_inc(h_ready, 1)

            def split(s):
                for c in range(N // 512):
                    i = 8 * s + c
                    cols = slice(512 * c, 512 * (c + 1))
                    dve.wait_ge(qk_ready, i + 1)
                    qp, kp = lg[c % 2][:, 0:512], lg[c % 2][:, 512:1024]
                    v_.tensor_scalar(qhi, qp, QS, None, ALU.mult)
                    op(v_.tensor_scalar(k_hi[:, cols], kp, QS, None, ALU.mult))
                    v_.tensor_copy(q16[0:64, cols], qhi[0:64, :])
                    v_.scalar_tensor_tensor(q16[64:128, cols], qp[64:128, :], QS, qhi[64:128, :], ALU.mult, ALU.subtract)
                    v_.scalar_tensor_tensor(k_lo[:, cols], kp, QS, k_hi[:, cols], ALU.mult, ALU.subtract
                                            ).then_inc(qk_split, 1)
                    dve.drain()
                op(v_.tensor_reduce(ks[:], k_hi[:], AX.X, ALU.add))
                v_.tensor_scalar(ks16[:], ks[:], 1.0 / N, None, ALU.mult).then_inc(mean_key, 1)
                dve.wait_ge(mean_logits, s + 1)
                v_.tensor_scalar(mu_row[:], sacc[:, 0:T], LS, None, ALU.mult).then_inc(mean_read, 1)
                dve.drain()

            def evacuate(s, pr, k):
                gp = s * PAIRS + pr
                for v in range(2):
                    for c in range(NCH):
                        i = v * NCH + c
                        dve.wait_ge(logits_ready, 2 * NCH * gp + i + 1)
                        v_.tensor_scalar(e[k][v][:, CH * c:CH * (c + 1)], lg[i % 2][:], 1.0, None, ALU.mult, ALU.max,
                                         accum_out=mx[:, i:i + 1]).then_inc(logits_read, 1)
                dve.drain()
                m = stat[k]
                op(v_.tensor_reduce(sm[:, 60:62], mx[:].rearrange("p (v c) -> p v c", c=NCH), AX.X, ALU.max))
                op(v_.tensor_scalar(m["negm"][:], sm[:, 60:62], -LS, None, ALU.mult))
                v_.tensor_tensor(m["mu"][:], mu_row[:, bass.ds(2 * pr, 2)], m["negm"][:], ALU.add).then_inc(max_ready, 1)
                dve.drain()

            c3 = cand[:].rearrange("p (v s m) -> p v s m", v=2, m=8)
            LH, V8, TC, OK, DONE, TS, LOB, HIB, HI, A1, A2, A3, PAR = (sm[:, 2 * i:2 * i + 2] for i in range(13))

            def window(k):
                for v in range(2):
                    for c in range(NWC):
                        w, cols = win[c % 2], slice(WC * c, WC * (c + 1))
                        op(v_.scalar_tensor_tensor(w[:], e[k][v][:, cols], HI[:, v:v + 1], e[k][v][:, cols], ALU.is_lt,
                                                   ALU.mult, accum_out=lh[:, NWC * v + c:NWC * v + c + 1]))
                        for sg in range(WC // SEG):
                            v_.max(c3[:, v, WC // SEG * c + sg, :], w[:, SEG * sg:SEG * (sg + 1)])
                v_.tensor_reduce(LH, lh[:].rearrange("p (v c) -> p v c", v=2), AX.X, ALU.add)
                dve.drain()

            def window_search(k):
                d = stat[k]["d"]
                v_.tensor_reduce(V8, c3[:, :, :, 7], AX.X, ALU.max)
                for r in range(ROUNDS):
                    for v in range(2):
                        v_.max(top[:, NTOP * v + 8 * r:NTOP * v + 8 * (r + 1)], cand[:, NSEG * 8 * v:NSEG * 8 * (v + 1)])
                    dve.drain()
                    if r < ROUNDS - 1:
                        for v in range(2):
                            cv = cand[:, NSEG * 8 * v:NSEG * 8 * (v + 1)]
                            v_.match_replace(cv, top[:, NTOP * v + 8 * r:NTOP * v + 8 * (r + 1)], cv, -1.0)
                        dve.drain()
                for v in range(2):
                    c = slice(NTOP * v, NTOP * (v + 1))
                    v_.tensor_tensor_scan(pre[:, c], ones[:], top[:, c], LH[:, v:v + 1], ALU.mult, ALU.subtract)
                dve.drain()
                for v in range(2):
                    c = slice(NTOP * v, NTOP * (v + 1))
                    v_.scalar_tensor_tensor(wn[:, c], pre[:, c], d[:, v:v + 1], top[:, c], ALU.is_le, ALU.mult)
                v_.tensor_tensor(A1, LH, d[:], ALU.is_gt)
                dve.drain()
                op(v_.tensor_reduce(TC, wn[:].rearrange("p (v c) -> p v c", v=2), AX.X, ALU.max))
                op(v_.tensor_tensor(A2, TC, V8, ALU.is_gt))
                op(v_.tensor_tensor(OK, A1, A2, ALU.mult))

            def open_rows(reg, OK_ALL):
                op(v_.tensor_tensor(flag[:, 0:1], OK_ALL[:, 0:1], OK_ALL[:, 1:2], ALU.mult))
                op(v_.transpose(flag_t[:], flag[:]))
                op(v_.tensor_reduce(flag_t[:, 0:1], flag_t[:, 0:32], AX.X, ALU.min))
                for q in range(1, 4):
                    v_.tensor_copy(flag_t[0:1, q:q + 1], flag_t[32 * q:32 * q + 1, 0:1])
                dve.drain()
                op(v_.tensor_reduce(flag_i[0:1, 0:1], flag_t[0:1, 0:4], AX.X, ALU.min))
                dve.load(reg, flag_i[0:1, 0:1])

            def retry(k, reg):
                m = stat[k]
                d, q = m["d"][:], m["q"][:]
                op(v_.tensor_tensor(A1, LH, d, ALU.is_gt))
                op(v_.tensor_scalar(A2, A1, -4.0, 4.0, ALU.mult, ALU.add))
                op(v_.tensor_tensor(A2, A2, HI, ALU.add))
                op(v_.tensor_tensor(HIB, HIB, A2, ALU.min))
                op(v_.tensor_scalar(A1, A1, -1.0, 1.0, ALU.mult, ALU.add))
                op(v_.tensor_tensor(A1, A1, HI, ALU.mult))
                op(v_.tensor_tensor(LOB, LOB, A1, ALU.max))
                op(v_.reciprocal(A1, HI))
                op(v_.tensor_tensor(A2, d, LH, ALU.subtract))
                op(v_.tensor_tensor(A1, A1, A2, ALU.mult))
                op(v_.tensor_scalar(A1, A1, 1.0 / KQ, SHIFT / KQ, ALU.mult, ALU.add))
                op(v_.tensor_tensor(A1, A1, q, ALU.mult))
                op(v_.tensor_tensor(A1, A1, HI, ALU.add))
                op(v_.tensor_tensor(A2, LOB, HIB, ALU.add))
                op(v_.tensor_scalar(A2, A2, 0.5, None, ALU.mult))
                op(v_.tensor_scalar(PAR, PAR, -1.0, 1.0, ALU.mult, ALU.add))
                op(v_.tensor_tensor(A3, A1, LOB, ALU.is_gt))
                op(v_.tensor_tensor(A3, A3, PAR, ALU.mult))
                op(v_.tensor_tensor(OK, A1, HIB, ALU.is_lt))
                op(v_.tensor_tensor(A3, A3, OK, ALU.mult))
                op(v_.tensor_tensor(A1, A1, A2, ALU.subtract))
                op(v_.tensor_tensor(A1, A1, A3, ALU.mult))
                op(v_.tensor_tensor(HI, A1, A2, ALU.add))
                window(k)
                window_search(k)
                settle()
                op(v_.scalar_tensor_tensor(A1, LOB, EPS_COLLAPSE, HIB, ALU.mult, ALU.is_ge))
                op(v_.tensor_scalar(A2, DONE, -1.0, 1.0, ALU.mult, ALU.add))
                op(v_.tensor_tensor(A1, A1, A2, ALU.mult))
                op(v_.tensor_tensor(A2, A1, LOB, ALU.mult))
                op(v_.tensor_tensor(TS, TS, A2, ALU.add))
                op(v_.tensor_tensor(DONE, DONE, A1, ALU.add))
                open_rows(reg, DONE)

            def settle():
                op(v_.tensor_scalar(A1, DONE, -1.0, 1.0, ALU.mult, ALU.add))
                op(v_.tensor_tensor(A1, A1, OK, ALU.mult))
                op(v_.tensor_tensor(A2, A1, TC, ALU.mult))
                op(v_.tensor_tensor(TS, TS, A2, ALU.add))
                op(v_.tensor_tensor(DONE, DONE, A1, ALU.add))

            def attended(s, pr, u):
                gp = s * PAIRS + pr
                dve.wait_ge(tiles_used, 16 * gp + 16)
                dst = xaE if s == 0 else hE
                for v in range(2):
                    v_.reciprocal(sm[:, 40 + v:41 + v], pv[:, DE * v + D:DE * v + D + 1])
                if u == 0:
                    v_.tensor_copy(half[:, 0:D + 1 if s == 0 else D], pv[:, RS:RS + (D + 1 if s == 0 else D)])
                dve.drain()
                for v in range(2):
                    last = v_.tensor_scalar(row_tile(dst, 2 * pr + v), pv[:, DE * v:DE * v + D], sm[:, 40 + v:41 + v],
                                            None, ALU.mult)
                last.then_inc(pv_read, 1)
                dve.drain()

            def scaled(s, g):
                dve.wait_ge(adj_used[1], (s * GROUPS + g + 1) * NSC)
                w = fw[s]
                prev = src_f[s][:, bass.ds(g * (4 * w), 4 * w)].rearrange("p (t d) -> p t d", d=w)[:, :, 0:D]
                dst = xf[:, bass.ds(g * (4 * D), 4 * D)] if s == 0 else rx_group[:]
                z3 = sacc[:, 0:3 * DE].rearrange("p (t d) -> p t d", d=DE)
                t3 = by_tile(rx_group[:], 4)
                if s == 0:
                    v_.tensor_scalar(rs[:, 0:3], z3[:, :, D], 1.0, None, ALU.add)
                    v_.scalar_tensor_tensor(rs[:, 3:4], pv[:, RS + D:RS + D + 1], 1.0, half[:, D:D + 1], ALU.add, ALU.add)
                else:
                    if not isinstance(g, int) or g > 0:
                        dve.wait_ge(rx_stored, 16 * g)
                v_.tensor_tensor(t3[:, 0:3, :], z3[:, :, 0:D], prev[:, 0:3, :], ALU.add)
                op(v_.tensor_tensor(t3[:, 3, :], prop(3), prev[:, 3, :], ALU.add))
                v_.tensor_tensor(t3[:, 3, :], t3[:, 3, :], half[:, 0:D], ALU.add)
                dve.drain()
                if s == 0:
                    op(v_.reciprocal(rinv[:, bass.ds(g * 4, 4)], rs[:, 0:4]))
                v_.tensor_tensor(by_tile(dst, 4), t3, rinv[:, bass.ds(g * 4, 4)].unsqueeze(2).broadcast_to([P, 4, D]),
                                 ALU.mult).then_inc(rx_ready, 1)
                dve.drain()

            def finish(s, pr, k, reg, between):
                gp = s * PAIRS + pr
                m = stat[k]
                dve.wait_ge(threshold_ready, thresholds_before(s, pr + 1))
                v_.tensor_copy(HI, m["hi"][:])
                v_.memset(PAR, 0.0)
                v_.tensor_scalar(LOB, m["d"][:], 0.5 / N, None, ALU.mult)
                v_.memset(HIB, 2.5)
                dve.drain()
                window(k)
                between()
                window_search(k)
                v_.tensor_copy(DONE, OK)
                v_.tensor_tensor(TS, OK, TC, ALU.mult)
                open_rows(reg, OK)
                with dve.While(lambda: dve.snap(reg) < 1):
                    retry(k, reg)
                if s > 0 or not isinstance(pr, int) or pr > 0:
                    dve.wait_ge(tiles_transposed, 16 * gp)
                for v in range(2):
                    v_.scalar_tensor_tensor(pm[v][:], e[k][v][:], TS[:, v:v + 1], e[k][v][:], ALU.is_ge, ALU.mult
                                            ).then_inc(masked, 1)
                dve.drain()

            def features_again():
                dve.wait_ge(x_loaded, 32)
                h3, mean = by_tile(h2[:]), st32[:, 0:T]
                op(v_.tensor_copy(h2[:], x_fin[:]))
                op(v_.tensor_reduce(mean, h3, AX.X, ALU.add))
                op(v_.tensor_scalar(mean, mean, 1.0 / D, None, ALU.mult))
                op(v_.tensor_tensor(h3, h3, mean.unsqueeze(2).broadcast_to([P, T, D]), ALU.subtract))
                op(v_.tensor_tensor(sq[:], h2[:], h2[:], ALU.mult))
                v_.tensor_reduce(st32[:, 2 * T:3 * T], by_tile(sq[:]), AX.X, ALU.add).then_inc(ln_variance, 1)
                dve.wait_ge(ln_rstd, 2)
                op(v_.scalar_tensor_tensor(h3, h3, 0.0, rstd_b, ALU.max, ALU.mult))

            reg = dve.alloc_register("open_rows")
            v_.memset(flag[:], 0.0)
            v_.memset(ones[:], 1.0)
            for buf in (hE, xaE):
                last = v_.memset(by_tile(buf[:], T, DE)[:, :, D:DE], 1.0)
            last.then_inc(ones_ready, 1)
            dve.wait_ge(x_loaded, 16)
            ln_centre(0, e[0][0][:])
            ln_var(0, pm[0][:])
            relu_rows(by_tile(hE[:], T, DE)[:, :, 0:D], e[0][0][:])
            dve.drain()
            for s in range(STEPS):
                split(s)
                evacuate(s, 0, 0)
                evacuate(s, 1, 1)

                def group(g, first=False, last=False):
                    for u in range(2):
                        pr = 2 * g + u

                        def between():
                            if not (first and u == 0):
                                attended(s, pr - 1, 1 - u)
                            if u == 0 and not first:
                                scaled(s, g - 1)
                        finish(s, pr, u, reg, between)
                        if not last:
                            evacuate(s, pr + 2, u)
                group(0, first=True)
                with dve.Fori(1, GROUPS - 1) as g:
                    group(g)
                group(GROUPS - 1, last=True)
                if s == STEPS - 1:
                    features_again()
                attended(s, PAIRS - 1, 1)
                scaled(s, GROUPS - 1)
            def centred(g):
                c = slice(512 * g, 512 * (g + 1))
                h3, s3 = by_tile(h2[:, c], 4), by_tile(sq[:, c], 4)
                mean = st32[:, 4 * g:4 * (g + 1)]
                dve.wait_ge(fin_product, g + 1)
                v_.tensor_tensor(h2[:, c], h2[:, c], lg[g % 2][:, 0:512], ALU.add).then_inc(fin_read, 1)
                dve.drain()
                op(v_.tensor_reduce(mean, h3, AX.X, ALU.add))
                op(v_.tensor_scalar(mean, mean, 1.0 / D, None, ALU.mult))
                op(v_.tensor_tensor(h3, h3, mean.unsqueeze(2).broadcast_to([P, 4, D]), ALU.subtract))
                op(v_.tensor_tensor(s3, h3, h3, ALU.mult))
                v_.tensor_reduce(st32[:, 2 * T + 4 * g:2 * T + 4 * (g + 1)], s3, AX.X, ALU.add).then_inc(ln_variance, 1)

            def normed(g):
                c = slice(512 * g, 512 * (g + 1))
                h3 = by_tile(h2[:, c], 4)
                rstd = st32[:, 2 * T + 4 * g:2 * T + 4 * (g + 1)].unsqueeze(2).broadcast_to([P, 4, D])
                dve.wait_ge(ln_rstd, 3 + g)
                op(v_.tensor_tensor(h3, h3, rstd, ALU.mult))
                op(v_.tensor_tensor(h3, h3, gsb.unsqueeze(1).broadcast_to([P, 4, D]), ALU.mult))
                op(v_.tensor_tensor(h3, h3, bsb.unsqueeze(1).broadcast_to([P, 4, D]), ALU.add))
                v_.tensor_tensor(h2[:, c], h2[:, c], x_fin[:, c], ALU.add).then_inc(fin_rows, 1)

            dve.wait_ge(final_loaded, 16 * FIN_LOADS)
            for g in range(GROUPS):
                centred(g)
                if g > 0:
                    normed(g - 1)
            normed(GROUPS - 1)

        @block.tensor
        def _(pe):
            mm, tr = nc.tensor.matmul, nc.tensor.transpose

            def setup(s):
                if s == 0:
                    pe.wait_ge(weights_loaded, 64)
                    pe.wait_ge(ones_ready, 1)
                    pe.wait_ge(h_ready, 1)
                else:
                    pe.wait_ge(pv_read, PAIRS)
                    pe.wait_ge(rx_ready, GROUPS)
                chunks = N // 512

                def transposes(c):
                    i = chunks * s + c
                    if c >= 2:
                        pe.wait_ge(xt_copied, i - 1)
                    for m in range(4):
                        last = tr(aux[c % 2][:, P * m:P * (m + 1)], row_tile(srcE[s], 4 * c + m), ident[:])
                    last.then_inc(x_transposed, 1)

                transposes(0)
                transposes(1)
                for c in range(chunks):
                    i = chunks * s + c
                    pe.wait_ge(xt_copied, i + 1)
                    if i > 0:
                        pe.wait_ge(q1_copied, i)
                    mm(sacc[0:64, :], w1[:], pt[c % 2][:], start=True, stop=True).then_inc(q1_ready, 1)
                    if c >= 2:
                        pe.wait_ge(qk_split, i - 1)
                    mm(lg[c % 2][:, 512:1024], w3[:], pt[c % 2][:], start=True, stop=True)
                    if c + 2 < chunks:
                        transposes(c + 2)
                    pe.wait_ge(q1_copied, i + 1)
                    mm(lg[c % 2][:, 0:512], w2[:], q1s, start=True, stop=True).then_inc(qk_ready, 1)
                pe.wait_ge(mean_key, s + 1)
                for t in range(T):
                    last = mm(sacc[:, t:t + 1], q16[:, P * t:P * (t + 1)], ks16[:], start=True, stop=True)
                last.then_inc(mean_logits, 1)
                pe.wait_ge(mean_read, s + 1)

            def logits(s, pr, i):
                v, c = divmod(i, NCH)
                idx = 2 * NCH * (s * PAIRS + pr) + i
                if s > 0 or i >= 2 or not isinstance(pr, int) or pr > 0:
                    pe.wait_ge(logits_read, idx - 1)
                q = q16[:, bass.ds((2 * pr + v) * P, P)]
                for h in range(2):
                    o = lg[i % 2][:, 512 * h:512 * (h + 1)]
                    cols = slice(CH * c + 512 * h, CH * c + 512 * (h + 1))
                    mm(o, q, k_hi[:, cols], start=True, stop=False)
                    last = mm(o, q, k_lo[:, cols], start=False, stop=True)
                last.then_inc(logits_ready, 1)

            def propagate(s, g, u):
                if u == 0 and (not isinstance(g, int) or g > 0):
                    pe.wait_ge(rx_ready, s * GROUPS + g)
                w = D + 1 if s == 0 else D
                for c in range(NSC):
                    cc = NSC * u + c
                    i = cc % 2
                    pe.wait_ge(adj_loaded[i], 16 * ((s * GROUPS + g) * NSC + cc // 2 + 1))
                    for j in range(SJ):
                        n = cc * SJ + j
                        for m in range(4):
                            last = mm(prop(m, w), s_ring[i][:, 512 * j + P * m:512 * j + P * (m + 1)],
                                      src_f[s][:, n * fw[s]:n * fw[s] + w],
                                      start=n == 0 and m == 0 or c == j == 0 and m == 3,
                                      stop=n == T - 1 or m == 3 and c == NSC - 1 and j == SJ - 1,
                                      skip_group_check=True)
                    last.then_inc(adj_used[i], 1)

            def attend(s, pr, v, q):
                idx = 16 * (s * PAIRS + pr) + 8 * v + q
                pe.wait_ge(tiles_copied, idx + 1)
                for j in range(4):
                    t = 4 * q + j
                    last = mm(pv[:, DE * v:DE * v + D + 1], pt[q % 2][:, P * j:P * (j + 1)],
                              row_tile(srcE[s], t, D + 1), start=t == 0, stop=t == T - 1)
                last.then_inc(tiles_used, 1)

            def iteration(s, g, u, last_group=False):
                pr = 2 * g + u
                gp = s * PAIRS + pr
                started = s > 0 or u > 0 or not isinstance(g, int) or g > 0
                if not last_group:
                    logits(s, pr + 2, 0)
                    logits(s, pr + 2, 1)
                if started:
                    pe.wait_ge(pv_read, gp)
                propagate(s, g, u)
                for n in range(16):
                    v, q = divmod(n, 8)
                    if q == 0:
                        pe.wait_ge(masked, 2 * gp + v + 1)
                    if started or n >= 2:
                        pe.wait_ge(tiles_copied, 16 * gp + n - 1)
                    for m in range(4):
                        t = 4 * q + m
                        last = tr(aux[q % 2][:, P * m:P * (m + 1)], pm[v][:, P * t:P * (t + 1)], ident[:])
                    last.then_inc(tiles_transposed, 1)
                    if n in (1, 2, 3) and not last_group:
                        logits(s, pr + 2, 2 * n)
                        logits(s, pr + 2, 2 * n + 1)
                    if n > 0:
                        attend(s, pr, *divmod(n - 1, 8))
                attend(s, pr, 1, 7)

            for s in range(STEPS):
                setup(s)
                for pr in range(2):
                    for i in range(2 * NCH):
                        logits(s, pr, i)
                for u in range(2):
                    iteration(s, 0, u)
                with pe.Fori(1, GROUPS - 1) as g:
                    for u in range(2):
                        iteration(s, g, u)
                for u in range(2):
                    iteration(s, GROUPS - 1, u, last_group=True)
            pe.wait_ge(final_loaded, 16 * FIN_LOADS)
            pe.wait_ge(pv_read, 2 * PAIRS)
            pe.wait_ge(rx_ready, 2 * GROUPS)
            rows = ((xf, D), (xaE, DE), (fin_src, D), (hE, DE))
            for g in range(GROUPS):
                for a, (src, w) in enumerate(rows):
                    i = 4 * g + a
                    if i >= 2:
                        pe.wait_ge(fin_copied, i - 1)
                    for m in range(4):
                        t = 4 * g + m
                        tile = src[:, w * t:w * t + D]
                        if src is fin_src and g == GROUPS - 1:
                            tile = rx_group[:, D * m:D * (m + 1)]
                        last = tr(aux[a % 2][:, P * m:P * (m + 1)], tile, ident[:])
                    last.then_inc(fin_transposed, 1)
                pe.wait_ge(fin_copied, 4 * g + 4)
                if g >= 2:
                    pe.wait_ge(fin_read, g - 1)
                for m in range(4):
                    for a in range(4):
                        last = mm(lg[g % 2][:, P * m:P * (m + 1)], FT[a][:, P * m:P * (m + 1)], us[a],
                                  start=a == 0, stop=a == 3)
                last.then_inc(fin_product, 1)

    return nc


_IN = ["x", "adj_t", "w1_t", "w2_tt", "w3_tt", "u_t", "gain", "shift", "ident"]


def kernel(x, adj, L0_gnn_W1, L0_gnn_W2, L0_gnn_W3, L0_gnn_U1, L0_gnn_U2, L0_gnn_ln_g, L0_gnn_ln_b):
    import numpy as np
    import concourse.bacc as bacc
    from concourse import mybir
    from concourse.bass_utils import run_bass_kernel_spmd

    c = np.ascontiguousarray
    x, adj, w1, w2, w3, u1, u2 = (np.asarray(a) for a in (x, adj, L0_gnn_W1, L0_gnn_W2, L0_gnn_W3, L0_gnn_U1, L0_gnn_U2))
    n = x.shape[0]
    adj_t = c(adj.reshape(n // 512, 512, n // 256, 2, 128).transpose(0, 2, 4, 3, 1)).reshape(n // 512, n // 256, 128, 1024)
    arrays = {
        "x": c(x), "adj_t": adj_t, "w1_t": c(w1.T),
        "w2_tt": c(np.concatenate([w2.T, w2.T], 1)), "w3_tt": c(np.concatenate([w3.T, w3.T], 1)),
        "u_t": c(np.stack([u1[0].T, u2[0].T, u1[1].T, u2[1].T])),
        "gain": c(np.broadcast_to(np.asarray(L0_gnn_ln_g), (128, x.shape[1]))),
        "shift": c(np.broadcast_to(np.asarray(L0_gnn_ln_b), (128, x.shape[1]))),
        "ident": np.eye(128, dtype=np.float32),
    }
    nc = bacc.Bacc("TRN2", target_bir_lowering=False, num_devices=1)
    args = [nc.dram_tensor(f"in_{k}", arrays[k].shape, mybir.dt.from_np(arrays[k].dtype), kind="ExternalInput").ap()
            for k in _IN]
    out = nc.dram_tensor("out_0", x.shape, mybir.dt.float32, kind="ExternalOutput").ap()
    rows = nc.dram_tensor("xf_rows", (n // 512, 128, 512), mybir.dt.float32, kind="Internal").ap()
    top_p_graph_mix(nc, *args, out, rows)
    r = run_bass_kernel_spmd(nc, [{f"in_{k}": arrays[k] for k in _IN}], core_ids=[0])
    return r.results[0]["out_0"]
```
